# Optimizing a Trainium2 kernel written in Bass

```python
import numpy as np
import jax
import jax.numpy as jnp

def _softmax(x, axis=-1):
    return jax.nn.softmax(x, axis=axis)

def _gelu(x):
    return jax.nn.gelu(x, approximate=True)

def _silu(x):
    return jax.nn.silu(x)

def _sigmoid(x):
    return jax.nn.sigmoid(x)

def _layernorm(x, axis=-1, eps=1e-05):
    m = jnp.mean(x, axis=axis, keepdims=True)
    v = jnp.var(x, axis=axis, keepdims=True)
    return (x - m) / jnp.sqrt(v + eps)

def _scatter_add(tgt, idx, src, axis=0):
    return tgt.at[idx].add(src)

def _segment_sum(src, seg, n):
    return jax.ops.segment_sum(src, seg, n)
kernel_name = 'mk_gnn_resnorm_d2_gnn_r32_acc785'

def setup_inputs(seed: int=0):
    np.random.seed(seed)
    _w = jnp.asarray

    def _rec_inputs():
        import jax
        import jax.numpy as jnp
        _gk = jax.random.key(seed)
        x = -0.0009044 + 1 * jax.random.normal(jax.random.fold_in(_gk, 1), (3125, 32), jnp.float32)
        _s = jax.random.randint(jax.random.fold_in(_gk, 2), (25000,), 0, 3125, jnp.int32)
        _d = jax.random.randint(jax.random.fold_in(_gk, 3), (25000,), 0, 3125, jnp.int32)
        _loop = jnp.arange(3125, dtype=jnp.int32)
        src = jnp.concatenate([_s, _d, _loop])
        dst = jnp.concatenate([_d, _s, _loop])
        _o = jnp.argsort(dst, stable=True)
        src = src[_o]
        dst = dst[_o]
        edge_type_86 = jax.random.randint(jax.random.fold_in(_gk, 13), (53125,), 0, 86, jnp.int32)
        edge_weight = jax.random.uniform(jax.random.fold_in(_gk, 14), (53125,), jnp.float32, 0.0, 1)
        return (x, src, dst, edge_type_86, edge_weight)
    x, src, dst, edge_type_86, edge_weight = _rec_inputs()

    def _L0_gnn_setup():
        import jax, jax.numpy as jnp
        import numpy as np
        N_NODES = 50000
        N_EDGES = 25000
        INP_DIM = 32
        OUT_DIM = 32
        ATTN_DIM = 32
        NUM_RELS = 86
        NUM_BASES = 16
        GAMMA = 0.0
        key = jax.random.key(seed)
        ks = jax.random.split(key, 12)
        return {'h': jax.random.normal(ks[0], (N_NODES, INP_DIM), jnp.float32), 'weight': jax.random.normal(ks[1], (NUM_BASES, INP_DIM, OUT_DIM), jnp.float32), 'w_comp': jax.random.normal(ks[2], (NUM_RELS, NUM_BASES), jnp.float32), 'self_loop_weight': jax.random.normal(ks[3], (INP_DIM, OUT_DIM), jnp.float32), 'A1_w': jax.random.normal(ks[4], (ATTN_DIM, INP_DIM), jnp.float32), 'A1_b': jax.random.normal(ks[5], (ATTN_DIM,), jnp.float32), 'A2_w': jax.random.normal(ks[6], (ATTN_DIM, INP_DIM), jnp.float32), 'A2_b': jax.random.normal(ks[7], (ATTN_DIM,), jnp.float32), 'rel_emb': jax.random.normal(ks[8], (NUM_RELS, ATTN_DIM), jnp.float32), 'src': jax.random.randint(ks[9], (N_EDGES,), 0, N_NODES, jnp.int32), 'dst': jax.random.randint(ks[10], (N_EDGES,), 0, N_NODES, jnp.int32), 'etype': jax.random.randint(ks[11], (N_EDGES,), 0, NUM_RELS, jnp.int32)}
    _L0_gnn_all = _L0_gnn_setup()
    _L0_gnn_in = {k: v for k, v in _L0_gnn_all.items() if k in ('weight', 'w_comp', 'self_loop_weight', 'A1_w', 'A1_b', 'A2_w', 'A2_b', 'rel_emb')}
    del _L0_gnn_all

    def _L1_gnn_setup():
        import jax, jax.numpy as jnp
        import numpy as np
        N_NODES = 3125
        N_EDGES = 50000
        N_FEAT = 32
        key = jax.random.key(seed)
        k1, k2, k3, k4 = jax.random.split(key, 4)
        u = jax.random.normal(k1, (N_NODES, N_FEAT), dtype=jnp.float32)
        weights = jax.random.uniform(k2, (N_EDGES,), dtype=jnp.float32)
        row = jax.random.randint(k3, (N_EDGES,), 0, N_NODES)
        col = jax.random.randint(k4, (N_EDGES,), 0, N_NODES)
        edge_index = jnp.stack([row, col]).astype(jnp.int64)
        return {'u': u, 'weights': weights, 'edge_index': edge_index}
    _L1_gnn_all = _L1_gnn_setup()
    _L1_gnn_in = {k: v for k, v in _L1_gnn_all.items() if k in ()}
    del _L1_gnn_all
    return {'x': x, 'src': src, 'dst': dst, 'edge_type_86': edge_type_86, 'edge_weight': edge_weight, 'L0_gnn_weight': _L0_gnn_in['weight'], 'L0_gnn_w_comp': _L0_gnn_in['w_comp'], 'L0_gnn_self_loop_weight': _L0_gnn_in['self_loop_weight'], 'L0_gnn_A1_w': _L0_gnn_in['A1_w'], 'L0_gnn_A1_b': _L0_gnn_in['A1_b'], 'L0_gnn_A2_w': _L0_gnn_in['A2_w'], 'L0_gnn_A2_b': _L0_gnn_in['A2_b'], 'L0_gnn_rel_emb': _L0_gnn_in['rel_emb']}

def reference(x, src, dst, edge_type_86, edge_weight, L0_gnn_weight, L0_gnn_w_comp, L0_gnn_self_loop_weight, L0_gnn_A1_w, L0_gnn_A1_b, L0_gnn_A2_w, L0_gnn_A2_b, L0_gnn_rel_emb):
    import jax
    import jax.numpy as jnp

    def _L0_gnn_ref(h, weight, w_comp, self_loop_weight, A1_w, A1_b, A2_w, A2_b, rel_emb, src, dst, etype):
        import jax, jax.numpy as jnp
        import numpy as np
        N_NODES = 50000
        N_EDGES = 25000
        INP_DIM = 32
        OUT_DIM = 32
        ATTN_DIM = 32
        NUM_RELS = 86
        NUM_BASES = 16
        GAMMA = 0.0
        E = src.shape[0]
        N = h.shape[0]
        x = h[src]
        y = h[dst]
        c = w_comp[etype]
        xb = jnp.einsum('ei,bio->ebo', x, weight)
        msg = jnp.einsum('eb,ebo->eo', c, xb)
        x_hat = x @ A1_w.T + A1_b
        y_hat = y @ A2_w.T + A2_b + rel_emb[etype]
        scale = jnp.sqrt(jnp.asarray(INP_DIM, h.dtype))
        a = jnp.tanh(jax.nn.relu(jnp.sum(x_hat * y_hat, axis=-1) / scale))
        a = jnp.where(a > GAMMA, a, jnp.zeros_like(a))
        nei = jax.ops.segment_sum(a[:, None] * msg, dst, num_segments=N)
        last_e = jax.ops.segment_max(jnp.arange(E, dtype=jnp.int32), dst, num_segments=N)
        last_e = jnp.clip(last_e, 0, E - 1)
        curr = h[src[last_e]] @ self_loop_weight
        in_deg = jax.ops.segment_sum(jnp.ones((E,), h.dtype), dst, num_segments=N)
        h_new = jnp.where((in_deg > 0)[:, None], nei + curr, jnp.zeros_like(nei))
        return jax.nn.relu(h_new)

    def _L1_gnn_ref(u, weights, edge_index):
        import jax, jax.numpy as jnp
        import numpy as np
        N_NODES = 3125
        N_EDGES = 50000
        N_FEAT = 32
        row, col = (edge_index[0], edge_index[1])
        diff = u[col] - u[row]
        weighted_diff = weights[:, None] * diff
        laplacian = jax.ops.segment_sum(weighted_diff, row, num_segments=u.shape[0])
        return laplacian
    edge_index = jnp.stack([src, dst])
    x = _layernorm(x + _L0_gnn_ref(x, L0_gnn_weight, L0_gnn_w_comp, L0_gnn_self_loop_weight, L0_gnn_A1_w, L0_gnn_A1_b, L0_gnn_A2_w, L0_gnn_A2_b, L0_gnn_rel_emb, src, dst, edge_type_86), axis=-1)
    x = _layernorm(x + _L1_gnn_ref(x, edge_weight, edge_index), axis=-1)
    return x

_drawn_inputs = setup_inputs


def setup_inputs(seed=0):
    import zlib

    import numpy as np

    out = dict(_drawn_inputs(seed))
    spreads = {}
    factors = {}
    for name, (base, spread) in spreads.items():
        noise = np.random.default_rng([zlib.crc32(name.encode()), seed]).standard_normal(out[name].shape)
        drawn = base * np.exp(spread * noise) if base else spread * noise
        out[name] = jnp.asarray(drawn.astype(out[name].dtype))
    for name, factor in factors.items():
        out[name] = (out[name] * factor).astype(out[name].dtype)
    return out
```

```python
from contextlib import ExitStack

import numpy as np

import concourse.bass as bass
import concourse.mybir as mybir
from concourse.alu_op_type import AluOpType as ALU

F32 = mybir.dt.float32
BF16 = mybir.dt.bfloat16
I32 = mybir.dt.int32
U32 = mybir.dt.uint32
ACT = mybir.ActivationFunctionType
AX = mybir.AxisListType.X

P = 128
D = 32
NB = 16
EPS = 1e-5
SLOTS = 25
HALF = 13
HS = 2 * HALF
GC = 4
KT = NB * D // P
BPT = P // D
KEY = 4096
RECIP, SHIFT = 5243, 17
VW = HALF * D
MW = VW + HALF
LW = D + 1
SRCW = P + D
TABW = 3 * D


def graph_kernel(nc, x, src, dst, etype, weight, bases, w_comp, self_w, a1_w, a1_b, a2_w, a2_b, rel_emb, out):
    N, E, R = x.shape[0], src.shape[0], w_comp.shape[0]
    ROWS = N // SLOTS
    PAD = N
    assert N == ROWS * SLOTS and ROWS < P and MW == HALF * LW
    CH = -(-E // (P * GC)) * GC
    GROUPS = CH // GC
    NBLK = 4
    BR = CH // NBLK
    FULL = E // P
    TAIL = E - FULL * P
    LASTROWS = FULL - (NBLK - 1) * BR
    assert CH == BR * NBLK and LASTROWS == BR - 1 and GROUPS % 2 == 0
    NT = -(-SLOTS // 4)
    SQ = 5
    QS = SLOTS // SQ

    src_tab = nc.dram_tensor("src_tab", [P * SLOTS, SRCW], F32).ap()
    dst_tab = nc.dram_tensor("dst_tab", [P * SLOTS, D], F32).ap()
    self_tab = nc.dram_tensor("self_tab", [P * SLOTS, D], F32).ap()
    x1_tab = nc.dram_tensor("x1_tab", [P * SLOTS, LW], F32).ap()
    chunk_tab = nc.dram_tensor("chunk_tab", [CH, 2 * P], F32).ap()
    type_tab = nc.dram_tensor("type_tab", [CH, P], BF16).ap()

    ctx = ExitStack()
    with ctx:
        def sb(name, shape, dt=F32):
            return ctx.enter_context(nc.sbuf_tensor(name, shape, dt))

        def sem(name):
            return ctx.enter_context(nc.semaphore(name))

        def need(eng, s, n):
            if not (isinstance(n, int) and n <= 0):
                eng.wait_ge(s, n)

        ident_i = sb("ident_i", [P, P], I32)
        ident = sb("ident", [P, P])
        iota_k = sb("iota_k", [P, 2 * P])
        iota_lo = sb("iota_lo", [P, HALF])
        type_id = sb("type_id", [P, 1])
        rep_i = sb("rep_i", [3 * NB, NB, D], I32)
        rep = sb("rep", [3 * NB, KT * P], BF16)
        node_id = sb("node_id", [P, SLOTS])
        pos_key = sb("pos_key", [P, P])
        eps_t = sb("eps_t", [P, 1])
        zeros = sb("zeros", [P, P], BF16)
        zrow = sb("zrow", [P, 512], BF16)
        x_sb = sb("x_sb", [P, SLOTS, D])
        src_n = sb("src_n", [BR, NBLK, P], I32)
        dst_n = sb("dst_n", [BR, NBLK, P], I32)
        typ_n = sb("typ_n", [BR, NBLK, P], I32)
        wgt_n = sb("wgt_n", [BR, NBLK, P])
        src_nf = sb("src_nf", [BR, NBLK, P])
        chunk_n = sb("chunk_n", [BR, NBLK, 2 * P])
        typ_nb = sb("typ_nb", [BR, NBLK, P], BF16)
        idx_all = sb("idx_all", [P, 2, CH], U32)
        scratch = sb("scratch", [P, 4, 2 * CH])
        n_f, row_f, slot_f, half_f = (scratch[:, i, :].rearrange("p (a c) -> p a c", a=2) for i in range(4))
        keyed = scratch[:, :, :].rearrange("p i c -> p (i c)")[:, 0:SLOTS * P].rearrange("p (s e) -> p s e", s=SLOTS)
        q_i = sb("q_i", [P, 2, CH], I32)
        k_all = sb("k_all", [P, 2, CH])
        lo_all = sb("lo_all", [P, 2, CH])
        w_all = sb("w_all", [P, CH])
        small_raw = sb("small_raw", [R, 3 * NB])
        small_res = sb("small_res", [R, 2, 3 * NB])
        small_bf = sb("small_bf", [R, 3, 3 * NB], BF16)
        rel_p = sb("rel_p", [R, 3, D], BF16)
        comp_p = sb("comp_p", [R, 3, NB], BF16)
        base_w = sb("base_w", [P, KT, D])
        a_raw = sb("a_raw", [P, 2, D])
        prod_w = sb("prod_w", [P, 4, TABW])
        bias_t = sb("bias_t", [P, 2, D])
        xT = sb("xT", [P, NT, P])
        dst_rows = sb("dst_rows", [P, SLOTS, D])
        self_rows = sb("self_rows", [P, SLOTS, D])
        stage = [sb(f"stage{i}", [P, 2, GC], U32) for i in range(2)]
        types_b = [sb(f"types_b{i}", [R, GC * P], BF16) for i in range(2)]
        type_hot = [sb(f"type_hot{i}", [R, GC * P], BF16) for i in range(2)]
        gx = [sb(f"gx{i}", [P, GC, SRCW]) for i in range(2)]
        gy = [sb(f"gy{i}", [P, GC, D]) for i in range(2)]
        compT = [sb(f"compT{i}", [3 * NB, GC * P], BF16) for i in range(2)]
        xsT = [sb(f"xsT{i}", [P, GC * P]) for i in range(2)]
        z_rows = sb("z_rows", [P, SLOTS * 2 * P])
        z = [z_rows[:, i * KT * GC * P:(i + 1) * KT * GC * P].rearrange("p (k e) -> p k e", k=KT) for i in range(2)]
        rows = z_rows[:, :].rearrange("p (s e) -> p s e", s=SLOTS)
        yr = [sb(f"yr{i}", [P, GC, D]) for i in range(2)]
        prod = [sb(f"prod{i}", [P, GC, D]) for i in range(2)]
        score = [sb(f"score{i}", [P, GC]) for i in range(2)]
        score_r = [sb(f"score_r{i}", [P, GC]) for i in range(2)]
        att = [sb(f"att{i}", [P, GC]) for i in range(2)]
        att_lo = [sb(f"att_lo{i}", [P, GC, HALF]) for i in range(2)]
        row_hot = [sb(f"row_hot{i}", [P, GC, 2 * P]) for i in range(2)]
        spread = [sb(f"spread{i}", [P, GC, MW]) for i in range(2)]
        counts = sb("counts", [P, CH * HS])
        src_rows = counts[:, 0:SLOTS * SRCW].rearrange("p (s c) -> p s c", c=SRCW)
        before = sb("before", [P, 2, CH])
        last_f = sb("last_f", [P, SLOTS])
        last_chunk = sb("last_chunk", [P, SLOTS], U32)
        key_f = sb("key_f", [P, SLOTS])
        key_u = sb("key_u", [P, SLOTS], U32)
        last_src = sb("last_src", [P, SLOTS], U32)
        curr = sb("curr", [P, SLOTS, D])
        has_in = sb("has_in", [P, SLOTS])
        h0 = sb("h0", [P, SLOTS, D])
        h1 = sb("h1", [P, SLOTS, D])
        mean = sb("mean", [P, SLOTS])
        cen = sb("cen", [P, SLOTS, D])
        sq = sb("sq", [P, SLOTS, D])
        var = sb("var", [P, SLOTS])
        std = sb("std", [P, SLOTS])
        rstd = sb("rstd", [P, SLOTS])
        x1 = sb("x1", [P, SLOTS, LW])
        y_out = sb("y_out", [P, SLOTS, D])
        dst_stage = [sb(f"dst_stage{i}", [P, GC], U32) for i in range(2)]
        g1 = [sb(f"g1{i}", [P, GC, LW]) for i in range(2)]
        slot_hot = [sb(f"slot_hot{i}", [P, GC, HALF]) for i in range(2)]

        acc = ctx.enter_context(nc.psum_tensor("acc", [P, 2, 512], F32))
        rep_ps = ctx.enter_context(nc.psum_tensor("rep_ps", [P, 2, 512], F32))
        comp_ps = ctx.enter_context(nc.psum_tensor("comp_ps", [P, 512], F32))
        xs_ps = ctx.enter_context(nc.psum_tensor("xs_ps", [P, 512], F32))
        msg_ps = ctx.enter_context(nc.psum_tensor("msg_ps", [P, 2, GC, D], F32))
        rel_ps = ctx.enter_context(nc.psum_tensor("rel_ps", [P, 2, GC, D], F32))

        pool_const = sem("pool_const")
        dve_const = sem("dve_const")
        pads_set = sem("pads_set")
        idx_loaded = sem("idx_loaded")
        wgt_loaded = sem("wgt_loaded")
        x_loaded = sem("x_loaded")
        par_loaded = sem("par_loaded")
        small_loaded = sem("small_loaded")
        base_loaded = sem("base_loaded")
        types_stored = sem("types_stored")
        chunk_stored = sem("chunk_stored")
        src_stored = sem("src_stored")
        dst_stored = sem("dst_stored")
        self_stored = sem("self_stored")
        nat_ready = sem("nat_ready")
        typ_ready = sem("typ_ready")
        prep_pe = sem("prep_pe")
        xT_copied = sem("xT_copied")
        tab_ready = sem("tab_ready")
        idx_ready = sem("idx_ready")
        dve = sem("dve")
        parts_ready = sem("parts_ready")
        weights_ready = sem("weights_ready")
        types_loaded = [sem(f"types_loaded{i}") for i in range(2)]
        type_hot_ready = sem("type_hot_ready")
        staged = sem("staged")
        turns = sem("turns")
        gathered = [sem(f"gathered{i}") for i in range(2)]
        comp_ready = sem("comp_ready")
        comp_copied = sem("comp_copied")
        xs_ready = sem("xs_ready")
        xs_copied = sem("xs_copied")
        rel_ready = sem("rel_ready")
        rep_ready = sem("rep_ready")
        z_ready = sem("z_ready")
        msg_ready = sem("msg_ready")
        yr_ready = sem("yr_ready")
        prod_ready = sem("prod_ready")
        score_ready = sem("score_ready")
        relu_ready = sem("relu_ready")
        att_ready = sem("att_ready")
        lo_ready = sem("lo_ready")
        att_lo_ready = sem("att_lo_ready")
        hot_ready = sem("hot_ready")
        spread_ready = sem("spread_ready")
        scattered = sem("scattered")
        counted = sem("counted")
        last_ready = sem("last_ready")
        rows_in = [sem(f"rows_in{i}") for i in range(QS)]
        last_src_ready = sem("last_src_ready")
        curr_in = sem("curr_in")
        acc_read = sem("acc_read")
        acc_cleared = sem("acc_cleared")
        var_ready = sem("var_ready")
        std_ready = sem("std_ready")
        x1_ready = sem("x1_ready")
        x1_stored = sem("x1_stored")
        staged1 = sem("staged1")
        gathered1 = [sem(f"gathered1{i}") for i in range(2)]
        slot_ready1 = sem("slot_ready1")
        hot_ready1 = sem("hot_ready1")
        spread_ready1 = sem("spread_ready1")
        scattered1 = sem("scattered1")
        out_ready = sem("out_ready")
        out_stored = sem("out_stored")

        block = ctx.enter_context(nc.Block())

        def group_loop(first, last, step):
            def run(eng):
                t = first
                end = first + (last - first) // 2 * 2
                with eng.Fori(0, (end - first) // 2) as i:
                    for b in range(2):
                        step(2 * i + (first + b), (first + b) % 2)
                for t in range(end, last):
                    step(t, t % 2)
            return run

        @block.sync
        def _(sp):
            nblk = "(b r) e -> r b e"

            def load_edges(tile, ap, s):
                full = ap[0:(NBLK - 1) * BR * P].rearrange("(b r e) -> r b e", r=BR, e=P)
                sp.dma_start(tile[:, 0:NBLK - 1, :], full).then_inc(s, 16)
                rest = ap[(NBLK - 1) * BR * P:FULL * P].rearrange("(r e) -> r e", e=P)
                sp.dma_start(tile[0:LASTROWS, NBLK - 1, :], rest).then_inc(s, 16)
                sp.dma_start(tile[LASTROWS:BR, NBLK - 1, 0:TAIL],
                             ap[FULL * P:E].rearrange("(r e) -> r e", r=1)).then_inc(s, 16)

            sp.wait_ge(pads_set, 6)
            sp.dma_start(x_sb[0:ROWS, :, :], x.rearrange("(r s) f -> r s f", s=SLOTS)).then_inc(x_loaded, 16)
            load_edges(src_n, src, idx_loaded)
            load_edges(dst_n, dst, idx_loaded)
            load_edges(typ_n, etype, idx_loaded)
            load_edges(wgt_n, weight, wgt_loaded)
            for q in range(4):
                rs = slice(q * D, (q + 1) * D)
                sp.dma_start(a_raw[rs, 0, :], a1_w).then_inc(par_loaded, 16)
                sp.dma_start(a_raw[rs, 1, :], a2_w).then_inc(par_loaded, 16)
                sp.dma_start(prod_w[rs, q, 2 * D:3 * D], self_w).then_inc(par_loaded, 16)
            sp.dma_start(bias_t[:, 0, :], a1_b.rearrange("(r f) -> r f", r=1).to_broadcast([P, D])).then_inc(par_loaded, 16)
            sp.dma_start(bias_t[:, 1, :], a2_b.rearrange("(r f) -> r f", r=1).to_broadcast([P, D])).then_inc(par_loaded, 16)
            sp.dma_start(small_raw[:, 0:D], rel_emb).then_inc(small_loaded, 16)
            sp.dma_start(small_raw[:, D:D + NB], w_comp).then_inc(small_loaded, 16)
            sp.dma_start(base_w[:, :, :], bases.rearrange("b i o -> (b i) o").rearrange("(k m) o -> m k o", k=KT)
                         ).then_inc(base_loaded, 16)
            sp.wait_ge(typ_ready, 1)
            sp.dma_start(type_tab.rearrange(nblk, b=NBLK), typ_nb[:, :, :]).then_inc(types_stored, 16)
            sp.wait_ge(tab_ready, BPT + 3 * NT)
            for tab, tile, s in ((src_tab, src_rows, src_stored), (dst_tab, dst_rows, dst_stored),
                                 (self_tab, self_rows, self_stored)):
                sp.dma_start(tab.rearrange("(r s) f -> r (s f)", s=SLOTS),
                             tile[:, :, :].rearrange("p s f -> p (s f)")).then_inc(s, 16)
            sp.wait_ge(nat_ready, 2)
            sp.dma_start(chunk_tab.rearrange(nblk, b=NBLK), chunk_n[:, :, :]).then_inc(chunk_stored, 16)

            sp.wait_ge(types_stored, 16)

            def load_types(t, b):
                need(sp, type_hot_ready, t - 1)
                sp.dma_start(types_b[b][:, :],
                             type_tab[bass.ds(t * GC, GC), :].rearrange("(a c) e -> a (c e)", a=1).to_broadcast([R, GC * P])
                             ).then_inc(types_loaded[b], 16)

            load_types(0, 0)
            load_types(1, 1)
            group_loop(2, GROUPS, load_types)(sp)

            sp.wait_ge(x1_ready, 1)
            sp.dma_start(x1_tab.rearrange("(r s) f -> r (s f)", s=SLOTS),
                         x1[:, :, :].rearrange("p s f -> p (s f)")).then_inc(x1_stored, 16)
            sp.wait_ge(out_ready, 1)
            sp.dma_start(out.rearrange("(r s) f -> r (s f)", s=SLOTS),
                         y_out[0:ROWS, :, :].rearrange("p s f -> p (s f)")).then_inc(out_stored, 16)
            for s in (types_stored, chunk_stored, src_stored, dst_stored, self_stored, x1_stored, out_stored):
                sp.wait_ge(s, 16)

        @block.gpsimd
        def _(pool):
            g = nc.gpsimd
            small = dict(allow_small_or_imprecise_dtypes=True)
            g.iota(ident_i[:, :], [[1, P]], base=0, channel_multiplier=-1).then_inc(pool_const, 1)
            g.iota(rep_i[:, :, :], [[1, NB], [0, D]], base=0, channel_multiplier=-1).then_inc(pool_const, 1)
            g.iota(iota_k[:, :], [[1, 2 * P]], base=0, channel_multiplier=0, **small).then_inc(pool_const, 1)
            g.iota(iota_lo[:, :], [[1, HALF]], base=0, channel_multiplier=0, **small).then_inc(pool_const, 1)
            g.iota(type_id[:, :], [[0, 1]], base=0, channel_multiplier=1, **small).then_inc(pool_const, 1)
            g.iota(node_id[:, :], [[1, SLOTS]], base=0, channel_multiplier=SLOTS, **small).then_inc(pool_const, 1)
            g.iota(pos_key[:, :], [[KEY, P]], base=0, channel_multiplier=0, **small).then_inc(pool_const, 1)

            pool.wait_ge(src_stored, 16)
            pool.wait_ge(dst_stored, 16)
            pool.wait_ge(idx_ready, 1)

            def gather_group(t, b, done):
                need(pool, gathered[b], done)
                g.tensor_copy(stage[b][:, :, :], idx_all[:, :, bass.ds(t * GC, GC)]).then_inc(staged, 1)
                need(pool, score_ready, t - 1)
                need(pool, xs_ready, t - 1)
                pool.wait_ge(staged, t + 1)
                pool.sem_inc(turns, 1)
                for j in range(GC):
                    g.indirect_dma_start(gx[b][:, j, :], None, src_tab,
                                         bass.IndirectOffsetOnAxis(stage[b][:, 0, j:j + 1], 0)).then_inc(gathered[b], 16)
                    g.indirect_dma_start(gy[b][:, j, :], None, dst_tab,
                                         bass.IndirectOffsetOnAxis(stage[b][:, 1, j:j + 1], 0)).then_inc(gathered[b], 16)

            gather_group(0, 0, 0)
            gather_group(1, 1, 0)
            with pool.Fori(1, GROUPS // 2) as i:
                for b in range(2):
                    gather_group(2 * i + b, b, i * (32 * GC))

            pool.wait_ge(chunk_stored, 16)
            pool.wait_ge(self_stored, 16)
            pool.wait_ge(last_ready, 1)
            for s in range(SLOTS):
                g.indirect_dma_start(rows[:, s, :], None, chunk_tab,
                                     bass.IndirectOffsetOnAxis(last_chunk[:, s:s + 1], 0)).then_inc(rows_in[s // SQ], 16)
            for s in range(SLOTS):
                if s % SQ == 0:
                    pool.wait_ge(last_src_ready, s // SQ + 1)
                g.indirect_dma_start(curr[:, s, :], None, self_tab,
                                     bass.IndirectOffsetOnAxis(last_src[:, s:s + 1], 0)).then_inc(curr_in, 16)

            pool.wait_ge(x1_stored, 16)

            def gather_group1(t, b, done):
                need(pool, gathered1[b], done)
                g.tensor_copy(dst_stage[b][:, :], idx_all[:, 1, bass.ds(t * GC, GC)]).then_inc(staged1, 1)
                need(pool, spread_ready1, (t - 1) * GC)
                pool.wait_ge(staged1, t + 1)
                pool.sem_inc(turns, 1)
                for j in range(GC):
                    g.indirect_dma_start(g1[b][:, j, :], None, x1_tab,
                                         bass.IndirectOffsetOnAxis(dst_stage[b][:, j:j + 1], 0)).then_inc(gathered1[b], 16)

            gather_group1(0, 0, 0)
            gather_group1(1, 1, 0)
            with pool.Fori(1, GROUPS // 2) as i:
                for b in range(2):
                    gather_group1(2 * i + b, b, i * (16 * GC))

        @block.tensor
        def _(pe):
            te = nc.tensor
            pe.wait_ge(dve_const, 1)
            pe.wait_ge(nat_ready, 2)
            pe.wait_ge(wgt_loaded, 48)
            for ps, tile in ((acc[:, 0, :], src_nf[:, :, :]), (acc[:, 1, :], chunk_n[:, :, 0:P]),
                             (comp_ps[:, :], wgt_n[:, :, :])):
                for b in range(NBLK):
                    m = te.transpose(ps[:, b * BR:(b + 1) * BR], tile[:, b, :], ident[0:BR, 0:BR])
                m.then_inc(prep_pe, 1)
            pe.wait_ge(x_loaded, 16)
            pe.wait_ge(weights_ready, 1)
            for j in range(NT):
                ns = min(4, SLOTS - 4 * j)
                if j >= 2:
                    pe.wait_ge(xT_copied, j - 1)
                te.transpose(xs_ps[0:ns * D, (j % 2) * P:(j % 2) * P + P],
                             x_sb[:, 4 * j:4 * j + ns, :].rearrange("p s f -> p (s f)"), ident[:, :]
                             ).then_inc(prep_pe, 1)
                pe.wait_ge(xT_copied, j + 1)
                if j >= 2:
                    pe.wait_ge(tab_ready, BPT + 3 * (j - 1))
                te.matmul(rep_ps[:, j % 2, 0:ns * TABW], xT[0:ns * D, j, :],
                          prod_w[0:ns * D, 0:ns, :].rearrange("p s c -> p (s c)"),
                          start=True, stop=True).then_inc(prep_pe, 1)
            pe.wait_ge(idx_ready, 1)
            for h in range(2):
                m = te.matmul(acc[:, h, 0:MW], zeros[:, :], zrow[:, 0:MW], start=True, stop=True)
            m.then_inc(acc_cleared, 1)
            pe.wait_ge(tab_ready, BPT + 3 * NT)
            pe.wait_ge(parts_ready, 1)
            pe.wait_ge(base_loaded, 16)

            def lookups(t, b, got):
                pe.wait_ge(type_hot_ready, t + 1)
                need(pe, comp_copied, t)
                te.matmul(comp_ps[0:3 * NB, :], comp_p[:, :, :].rearrange("r a c -> r (a c)"), type_hot[b][:, :],
                          start=True, stop=True).then_inc(comp_ready, 1)
                need(pe, xs_copied, t)
                pe.wait_ge(gathered[b], got)
                for j in range(GC):
                    m = te.transpose(xs_ps[:, j * P:(j + 1) * P], gx[b][:, j, 0:P], ident[:, :])
                m.then_inc(xs_ready, 1)
                need(pe, yr_ready, t - 1)
                for j in range(GC):
                    for a in range(3):
                        m = te.matmul(rel_ps[:, b, j, :], type_hot[b][:, j * P:(j + 1) * P], rel_p[:, a, :],
                                      start=(a == 0), stop=(a == 2))
                m.then_inc(rel_ready, 1)

            def repeat_comp(t, b, k):
                if k == 0:
                    pe.wait_ge(comp_copied, t + 1)
                need(pe, z_ready, t * KT + k - 1)
                te.matmul(rep_ps[:, k % 2, :], rep[:, k * P:(k + 1) * P], compT[b][:, :],
                          start=True, stop=True).then_inc(rep_ready, 1)

            def scatter(t, b, j):
                if j == 0:
                    pe.wait_ge(hot_ready, t + 1)
                pe.wait_ge(spread_ready, t * GC + j + 1)
                need(pe, counted, t * GC + j)
                for h in range(2):
                    m = te.matmul(acc[:, h, 0:MW], row_hot[b][:, j, h * P:(h + 1) * P], spread[b][:, j, :],
                                  start=False, stop=True, skip_group_check=True)
                m.then_inc(scattered, 1)

            def messages(t, b):
                pe.wait_ge(z_ready, (t + 1) * KT)
                for j in range(GC):
                    for k in range(KT):
                        m = te.matmul(msg_ps[:, b, j, :], z[b][:, k, j * P:(j + 1) * P], base_w[:, k, :],
                                      start=(k == 0), stop=(k == KT - 1))
                m.then_inc(msg_ready, 1)

            lookups(0, 0, 32 * GC)
            for k in range(KT):
                repeat_comp(0, 0, k)
            messages(0, 0)
            lookups(1, 1, 32 * GC)

            def slot(t, b, got):
                repeat_comp(t, b, 0)
                repeat_comp(t, b, 1)
                scatter(t - 1, 1 - b, 0)
                repeat_comp(t, b, 2)
                scatter(t - 1, 1 - b, 1)
                repeat_comp(t, b, 3)
                scatter(t - 1, 1 - b, 2)
                scatter(t - 1, 1 - b, 3)
                messages(t, b)
                if got is not None:
                    lookups(t + 1, 1 - b, got)

            with pe.Fori(0, GROUPS // 2 - 1) as i:
                slot(2 * i + 1, 1, (i + 2) * (32 * GC))
                slot(2 * i + 2, 0, (i + 2) * (32 * GC))
            slot(GROUPS - 1, 1, None)
            for j in range(GC):
                scatter(GROUPS - 1, 1, j)

            pe.wait_ge(acc_read, 1)
            pe.wait_ge(counted, CH)
            for h in range(2):
                m = te.matmul(acc[:, h, 0:MW], zeros[:, :], zrow[:, 0:MW], start=True, stop=True)
            m.then_inc(acc_cleared, 1)

            def scatter1(t, b):
                pe.wait_ge(hot_ready1, t + 1)
                for j in range(GC):
                    pe.wait_ge(spread_ready1, t * GC + (j + 1))
                    for h in range(2):
                        m = te.matmul(acc[:, h, 0:MW], row_hot[b][:, j, h * P:(h + 1) * P], spread[b][:, j, :],
                                      start=False, stop=True, skip_group_check=True)
                    m.then_inc(scattered1, 1)

            with pe.Fori(0, GROUPS // 2) as i:
                for b in range(2):
                    scatter1(2 * i + b, b)

        @block.scalar
        def _(act):
            sc = nc.scalar

            def copy_lookups(t, b):
                act.wait_ge(comp_ready, t + 1)
                need(act, rep_ready, (t - 1) * KT)
                sc.activation(compT[b][:, :], comp_ps[0:3 * NB, :], ACT.Copy).then_inc(comp_copied, 1)
                act.wait_ge(xs_ready, t + 1)
                need(act, z_ready, (t - 1) * KT)
                sc.activation(xsT[b][:, :], xs_ps[:, :], ACT.Copy).then_inc(xs_copied, 1)

            def count(t, j):
                c = t * GC + j
                act.wait_ge(scattered, c + 1)
                sc.activation(counts[:, bass.ds(c * HS, HS)].rearrange("p (h l) -> p h l", h=2),
                              acc[:, :, VW:MW], ACT.Copy).then_inc(counted, 1)

            def attention(t, b):
                act.wait_ge(score_ready, t + 1)
                sc.activation(score_r[b][:, :], score[b][:, :], ACT.Relu, scale=float(D) ** -0.5).then_inc(relu_ready, 1)
                act.wait_ge(relu_ready, t + 1)
                sc.activation(att[b][:, :], score_r[b][:, :], ACT.Tanh).then_inc(att_ready, 1)

            copy_lookups(0, 0)
            attention(0, 0)
            copy_lookups(1, 1)

            def slot(t, b, more):
                count(t - 1, 0)
                attention(t, b)
                count(t - 1, 1)
                count(t - 1, 2)
                count(t - 1, 3)
                if more:
                    copy_lookups(t + 1, 1 - b)

            with act.Fori(0, GROUPS // 2 - 1) as i:
                slot(2 * i + 1, 1, True)
                slot(2 * i + 2, 0, True)
            slot(GROUPS - 1, 1, False)
            for j in range(GC):
                count(GROUPS - 1, j)
            for n in range(2):
                act.wait_ge(var_ready, n + 1)
                sc.activation(std[:, :], var[:, :], ACT.Sqrt, bias=eps_t[:, 0:1], scale=1.0 / D).then_inc(std_ready, 1)

        @block.vector
        def _(ve):
            v = nc.vector
            done = [0]

            def link(ins):
                done[0] += 1
                ins.then_inc(dve, 1)
                ve.wait_ge(dve, done[0])

            def slots_b(ap, n=D):
                return ap.unsqueeze(2).to_broadcast([P, ap.shape[1], n])

            v.memset(src_n[:, NBLK - 1, :], PAD).then_inc(pads_set, 1)
            v.memset(dst_n[:, NBLK - 1, :], PAD).then_inc(pads_set, 1)
            v.memset(typ_n[:, NBLK - 1, :], 0).then_inc(pads_set, 1)
            v.memset(wgt_n[:, NBLK - 1, :], 0.0).then_inc(pads_set, 1)
            v.memset(x_sb[96:P, :, :], 0.0).then_inc(pads_set, 1)
            v.memset(zeros[:, :], 0.0)
            v.memset(zrow[:, :], 0.0)
            v.memset(eps_t[:, :], EPS)
            v.memset(x1[:, :, D:LW], 1.0)
            v.memset(prod_w[:, :, :], 0.0).then_inc(pads_set, 1)
            ve.wait_ge(pool_const, 7)
            v.tensor_scalar(ident[:, :], ident_i[:, :], 0.0, None, ALU.is_equal).then_inc(dve_const, 1)
            link(v.tensor_scalar(rep_i[:, :, :], rep_i[:, :, :], NB - 1, None, ALU.bitwise_and))
            link(v.tensor_scalar(rep[:, :], rep_i[:, :, :].rearrange("p b f -> p (b f)"), 0.0, None, ALU.is_equal))
            ve.wait_ge(idx_loaded, 3 * 48)
            v.tensor_copy(typ_nb[:, :, :], typ_n[:, :, :]).then_inc(typ_ready, 1)
            v.tensor_copy(chunk_n[:, :, 0:P], dst_n[:, :, :]).then_inc(nat_ready, 1)
            link(v.tensor_copy(src_nf[:, :, :], src_n[:, :, :]))
            v.tensor_tensor(chunk_n[:, :, P:2 * P], src_nf[:, :, :],
                            pos_key[0:BR, :].unsqueeze(1).to_broadcast([BR, NBLK, P]), ALU.add).then_inc(nat_ready, 1)
            ve.wait_ge(par_loaded, 14 * 16)
            for q in range(4):
                rs = slice(q * D, (q + 1) * D)
                v.transpose(prod_w[rs, q, 0:D], a_raw[rs, 0, :])
                m = v.transpose(prod_w[rs, q, D:2 * D], a_raw[rs, 1, :])
            m.then_inc(weights_ready, 1)
            ve.wait_ge(x_loaded, 16)
            for r in range(BPT):
                v.tensor_copy(src_rows[:, :, r * D:(r + 1) * D], x_sb[:, :, :]).then_inc(tab_ready, 1)
            for j in range(NT):
                ns = min(4, SLOTS - 4 * j)
                s = slice(4 * j, 4 * j + ns)
                ve.wait_ge(prep_pe, 4 + 2 * j)
                v.tensor_copy(xT[0:ns * D, j, :], xs_ps[0:ns * D, (j % 2) * P:(j % 2) * P + P]).then_inc(xT_copied, 1)
                ve.wait_ge(prep_pe, 5 + 2 * j)
                got = rep_ps[:, j % 2, 0:ns * TABW].rearrange("p (s c) -> p s c", c=TABW)
                bias = [bias_t[:, a, :].unsqueeze(1).to_broadcast([P, ns, D]) for a in range(2)]
                v.tensor_tensor(src_rows[:, s, P:SRCW], got[:, :, 0:D], bias[0], ALU.add).then_inc(tab_ready, 1)
                v.tensor_tensor(dst_rows[:, s, :], got[:, :, D:2 * D], bias[1], ALU.add).then_inc(tab_ready, 1)
                v.tensor_copy(self_rows[:, s, :], got[:, :, 2 * D:3 * D]).then_inc(tab_ready, 1)
            ve.wait_ge(prep_pe, 3)
            for a in range(2):
                v.tensor_copy(idx_all[:, a, :], acc[:, a, 0:CH])
                link(v.tensor_copy(n_f[:, a, :], acc[:, a, 0:CH]))
            v.tensor_copy(w_all[:, :], comp_ps[:, 0:CH])
            link(v.tensor_scalar(q_i[:, :, :], n_f[:, :, :], float(RECIP), None, ALU.mult))
            link(v.tensor_scalar(q_i[:, :, :], q_i[:, :, :], SHIFT, None, ALU.logical_shift_right))
            link(v.tensor_copy(row_f[:, :, :], q_i[:, :, :]))
            link(v.scalar_tensor_tensor(slot_f[:, :, :], row_f[:, :, :], -float(SLOTS), n_f[:, :, :], ALU.mult, ALU.add))
            link(v.tensor_scalar(half_f[:, :, :], slot_f[:, :, :], float(HALF), None, ALU.is_ge))
            link(v.scalar_tensor_tensor(k_all[:, :, :], half_f[:, :, :], float(P), row_f[:, :, :], ALU.mult, ALU.add))
            link(v.scalar_tensor_tensor(lo_all[:, :, :], half_f[:, :, :], -float(HALF), slot_f[:, :, :],
                                        ALU.mult, ALU.add))
            v.memset(has_in[:, :], 0.0).then_inc(idx_ready, 1)
            ve.wait_ge(small_loaded, 32)
            link(v.tensor_copy(small_bf[:, 0, :], small_raw[:, :]))
            link(v.tensor_tensor(small_res[:, 0, :], small_raw[:, :], small_bf[:, 0, :], ALU.subtract))
            link(v.tensor_copy(small_bf[:, 1, :], small_res[:, 0, :]))
            link(v.tensor_tensor(small_res[:, 1, :], small_res[:, 0, :], small_bf[:, 1, :], ALU.subtract))
            link(v.tensor_copy(small_bf[:, 2, :], small_res[:, 1, :]))
            v.tensor_copy(rel_p[:, :, :], small_bf[:, :, 0:D])
            link(v.tensor_copy(comp_p[:, :, :], small_bf[:, :, D:D + NB]))
            v.memset(last_f[:, :], 0.0).then_inc(parts_ready, 1)

            def type_one_hot(t, b, got):
                ve.wait_ge(types_loaded[b], got)
                need(ve, rel_ready, t - 1)
                v.tensor_scalar(type_hot[b][:, :], types_b[b][:, :], type_id[0:R, 0:1], None,
                                ALU.is_equal).then_inc(type_hot_ready, 1)

            def times_x(t, b, k):
                ve.wait_ge(rep_ready, t * KT + (k + 1))
                if k == 0:
                    ve.wait_ge(xs_copied, t + 1)
                    need(ve, msg_ready, t - 1)
                v.tensor_tensor(z[b][:, k, :], rep_ps[:, k % 2, :], xsT[b][:, :], ALU.mult).then_inc(z_ready, 1)

            def one_hots(t, b, a, hot, lo, hot_sem, lo_sem):
                c = bass.ds(t * GC, GC)
                v.tensor_tensor(lo, iota_lo[:, :].unsqueeze(1).to_broadcast([P, GC, HALF]),
                                lo_all[:, a, c].unsqueeze(2).to_broadcast([P, GC, HALF]),
                                ALU.is_equal).then_inc(lo_sem, 1)
                v.tensor_tensor(hot, iota_k[:, :].unsqueeze(1).to_broadcast([P, GC, 2 * P]),
                                k_all[:, a, c].unsqueeze(2).to_broadcast([P, GC, 2 * P]),
                                ALU.is_equal).then_inc(hot_sem, 1)

            def spread_msg(t, b, j):
                if j == 0:
                    ve.wait_ge(msg_ready, t + 1)
                    ve.wait_ge(att_lo_ready, t + 1)
                v.tensor_tensor(spread[b][:, j, 0:VW].rearrange("p (l f) -> p l f", f=D),
                                att_lo[b][:, j, :].unsqueeze(2).to_broadcast([P, HALF, D]),
                                msg_ps[:, b, j, :].unsqueeze(1).to_broadcast([P, HALF, D]),
                                ALU.mult).then_inc(spread_ready, 1)

            def slot(t, b, got, first=False):
                if not first:
                    spread_msg(t - 1, 1 - b, 0)
                times_x(t, b, 0)
                ve.wait_ge(rel_ready, t + 1)
                v.tensor_tensor(yr[b][:, :, :], rel_ps[:, b, :, :], gy[b][:, :, :], ALU.add).then_inc(yr_ready, 1)
                if not first:
                    spread_msg(t - 1, 1 - b, 1)
                ve.wait_ge(yr_ready, t + 1)
                v.tensor_tensor(prod[b][:, :, :], yr[b][:, :, :], gx[b][:, :, P:SRCW], ALU.mult).then_inc(prod_ready, 1)
                times_x(t, b, 1)
                ve.wait_ge(prod_ready, t + 1)
                need(ve, att_ready, t - 1)
                v.tensor_reduce(score[b][:, :], prod[b][:, :, :], AX, ALU.add).then_inc(score_ready, 1)
                if not first:
                    spread_msg(t - 1, 1 - b, 2)
                times_x(t, b, 2)
                need(ve, scattered, (t - 1) * GC)
                one_hots(t, b, 1, row_hot[b][:, :, :], spread[b][:, :, VW:MW], hot_ready, lo_ready)
                if not first:
                    spread_msg(t - 1, 1 - b, 3)
                times_x(t, b, 3)
                if got is not None:
                    type_one_hot(t + 1, 1 - b, got)
                ve.wait_ge(att_ready, t + 1)
                ve.wait_ge(lo_ready, t + 1)
                v.tensor_tensor(att_lo[b][:, :, :], spread[b][:, :, VW:MW],
                                att[b][:, :].unsqueeze(2).to_broadcast([P, GC, HALF]), ALU.mult).then_inc(att_lo_ready, 1)

            type_one_hot(0, 0, 16)
            ve.wait_ge(gathered[0], 32 * GC)
            slot(0, 0, 16, first=True)

            with ve.Fori(0, GROUPS // 2 - 1) as i:
                ve.wait_ge(gathered[1], (i + 1) * (32 * GC))
                slot(2 * i + 1, 1, i * 16 + 32)
                ve.wait_ge(gathered[0], (i + 2) * (32 * GC))
                slot(2 * i + 2, 0, i * 16 + 32)
            ve.wait_ge(gathered[1], (GROUPS // 2) * (32 * GC))
            slot(GROUPS - 1, 1, None)
            for j in range(GC):
                spread_msg(GROUPS - 1, 1, j)

            ve.wait_ge(counted, CH)
            cnt = counts[:, :].rearrange("p (c s) -> p s c", s=HS)
            for s in range(SLOTS):
                link(v.tensor_scalar(before[:, s % 2, :], cnt[:, s, :], counts[:, (CH - 1) * HS + s:(CH - 1) * HS + s + 1],
                                     0.0, ALU.is_lt, ALU.add, accum_out=last_f[:, s:s + 1]))
            v.tensor_copy(last_chunk[:, :], last_f[:, :]).then_inc(last_ready, 1)
            ve.wait_ge(scattered, CH)
            v.tensor_scalar(has_in[:, :], counts[:, (CH - 1) * HS:(CH - 1) * HS + SLOTS], 0.0, None, ALU.is_gt)
            v.tensor_copy(h0[:, 0:HALF, :], acc[:, 0, 0:VW].rearrange("p (l f) -> p l f", f=D))
            link(v.tensor_copy(h0[:, HALF:SLOTS, :],
                               acc[:, 1, 0:(SLOTS - HALF) * D].rearrange("p (l f) -> p l f", f=D)))
            v.memset(score[0][:, :], 0.0).then_inc(acc_read, 1)
            for q in range(QS):
                ss = slice(q * SQ, (q + 1) * SQ)
                ve.wait_ge(rows_in[q], 16 * SQ)
                for s in range(q * SQ, (q + 1) * SQ):
                    m = v.scalar_tensor_tensor(keyed[:, s, :], rows[:, s, 0:P], node_id[:, s:s + 1], rows[:, s, P:2 * P],
                                               ALU.is_equal, ALU.mult)
                link(m)
                link(v.tensor_reduce(key_f[:, ss], keyed[:, ss, :], AX, ALU.max))
                link(v.tensor_copy(key_u[:, ss], key_f[:, ss]))
                v.tensor_scalar(last_src[:, ss], key_u[:, ss], KEY - 1, None, ALU.bitwise_and).then_inc(last_src_ready, 1)

            def layer_norm(h, o, n):
                link(v.tensor_reduce(mean[:, :], h[:, :, :], AX, ALU.add))
                link(v.tensor_scalar(mean[:, :], mean[:, :], 1.0 / D, None, ALU.mult))
                link(v.tensor_tensor(cen[:, :, :], h[:, :, :], slots_b(mean[:, :]), ALU.subtract))
                link(v.tensor_tensor(sq[:, :, :], cen[:, :, :], cen[:, :, :], ALU.mult))
                v.tensor_reduce(var[:, :], sq[:, :, :], AX, ALU.add).then_inc(var_ready, 1)
                ve.wait_ge(std_ready, n)
                link(v.reciprocal(rstd[:, :], std[:, :]))
                link(v.tensor_tensor(o, cen[:, :, :], slots_b(rstd[:, :]), ALU.mult))

            ve.wait_ge(curr_in, 16 * SLOTS)
            link(v.tensor_tensor(h1[:, :, :], h0[:, :, :], curr[:, :, :], ALU.add))
            link(v.scalar_tensor_tensor(h0[:, :, :], h1[:, :, :], 0.0, slots_b(has_in[:, :]), ALU.max, ALU.mult))
            link(v.tensor_tensor(h1[:, :, :], h0[:, :, :], x_sb[:, :, :], ALU.add))
            layer_norm(h1, x1[:, :, 0:D], 1)
            v.memset(score[0][:, :], 0.0).then_inc(x1_ready, 1)

            def spread1(t, b, got, reuse):
                if reuse:
                    ve.wait_ge(scattered1, (t - 1) * GC)
                c = bass.ds(t * GC, GC)
                one_hots(t, b, 0, row_hot[b][:, :, :], slot_hot[b][:, :, :], hot_ready1, slot_ready1)
                ve.wait_ge(slot_ready1, t + 1)
                v.tensor_tensor(att_lo[b][:, :, :], slot_hot[b][:, :, :],
                                w_all[:, c].unsqueeze(2).to_broadcast([P, GC, HALF]), ALU.mult).then_inc(att_lo_ready, 1)
                ve.wait_ge(att_lo_ready, t + (GROUPS + 1))
                ve.wait_ge(gathered1[b], got)
                for j in range(GC):
                    v.tensor_tensor(spread[b][:, j, :].rearrange("p (l f) -> p l f", f=LW),
                                    att_lo[b][:, j, :].unsqueeze(2).to_broadcast([P, HALF, LW]),
                                    g1[b][:, j, :].unsqueeze(1).to_broadcast([P, HALF, LW]),
                                    ALU.mult).then_inc(spread_ready1, 1)

            spread1(0, 0, 16 * GC, False)
            spread1(1, 1, 16 * GC, False)
            with ve.Fori(1, GROUPS // 2) as i:
                for b in range(2):
                    spread1(2 * i + b, b, (i + 1) * (16 * GC), True)

            ve.wait_ge(scattered1, CH)
            for h, n in ((0, HALF), (1, SLOTS - HALF)):
                part = acc[:, h, 0:n * LW].rearrange("p (l f) -> p l f", f=LW)
                ss = slice(h * HALF, h * HALF + n)
                v.tensor_tensor(h0[:, ss, :], part[:, :, 0:D], x1[:, ss, 0:D], ALU.add)
                link(v.tensor_tensor(h1[:, ss, :], x1[:, ss, 0:D], part[:, :, D:LW].to_broadcast([P, n, D]), ALU.mult))
            link(v.tensor_tensor(h0[:, :, :], h0[:, :, :], h1[:, :, :], ALU.subtract))
            layer_norm(h0, y_out[:, :, :], 2)
            v.memset(score[0][:, :], 0.0).then_inc(out_ready, 1)


_INS = ["x", "src", "dst", "edge_type_86", "edge_weight", "L0_gnn_weight", "L0_gnn_w_comp", "L0_gnn_self_loop_weight",
        "L0_gnn_A1_w", "L0_gnn_A1_b", "L0_gnn_A2_w", "L0_gnn_A2_b", "L0_gnn_rel_emb"]


def kernel(**inputs):
    import numpy as _np
    import concourse.bacc as _bacc
    from concourse import mybir as _mybir
    from concourse.bass_utils import run_bass_kernel_spmd as _run

    nc = _bacc.Bacc("TRN2", target_bir_lowering=False, num_devices=1)
    arrays, args = {}, []
    for name in _INS:
        a = _np.ascontiguousarray(inputs[name])
        arrays[f"in_{name}_dram"] = a
        args.append(nc.dram_tensor(f"in_{name}_dram", a.shape, _mybir.dt.from_np(a.dtype), kind="ExternalInput").ap())
    shape = tuple(inputs["x"].shape)
    out = nc.dram_tensor("out_0_dram", shape, _mybir.dt.float32, kind="ExternalOutput").ap()
    graph_kernel(nc, *args, out)
    r = _run(nc, [arrays], core_ids=[0])
    return r.results[0]["out_0_dram"]
```

```python
from contextlib import ExitStack

import numpy as np

import concourse.bass as bass
import concourse.mybir as mybir
from concourse.alu_op_type import AluOpType as ALU

F32 = mybir.dt.float32
BF16 = mybir.dt.bfloat16
I32 = mybir.dt.int32
U32 = mybir.dt.uint32
ACT = mybir.ActivationFunctionType
AX = mybir.AxisListType.X

P = 128
D = 32
NB = 16
EPS = 1e-5
SLOTS = 25
HALF = 13
HS = 2 * HALF
GC = 4
KT = NB * D // P
BPT = P // D
KEY = 4096
RECIP, SHIFT = 5243, 17
VW = HALF * D
MW = VW + HALF
LW = D + 1
SRCW = P + D
TABW = 3 * D


def graph_kernel(nc, x, src, dst, etype, weight, bases, w_comp, self_w, a1_w, a1_b, a2_w, a2_b, rel_emb, out):
    N, E, R = x.shape[0], src.shape[0], w_comp.shape[0]
    ROWS = N // SLOTS
    PAD = N
    assert N == ROWS * SLOTS and ROWS < P and MW == HALF * LW
    CH = -(-E // (P * GC)) * GC
    GROUPS = CH // GC
    NBLK = 4
    BR = CH // NBLK
    FULL = E // P
    TAIL = E - FULL * P
    LASTROWS = FULL - (NBLK - 1) * BR
    assert CH == BR * NBLK and LASTROWS == BR - 1 and GROUPS % 2 == 0
    NT = -(-SLOTS // 4)
    SQ = 5
    QS = SLOTS // SQ

    src_tab = nc.dram_tensor("src_tab", [P * SLOTS, SRCW], F32).ap()
    dst_tab = nc.dram_tensor("dst_tab", [P * SLOTS, D], F32).ap()
    self_tab = nc.dram_tensor("self_tab", [P * SLOTS, D], F32).ap()
    x1_tab = nc.dram_tensor("x1_tab", [P * SLOTS, LW], F32).ap()
    chunk_tab = nc.dram_tensor("chunk_tab", [CH, 2 * P], F32).ap()
    type_tab = nc.dram_tensor("type_tab", [CH, P], BF16).ap()

    ctx = ExitStack()
    with ctx:
        def sb(name, shape, dt=F32):
            return ctx.enter_context(nc.sbuf_tensor(name, shape, dt))

        def sem(name):
            return ctx.enter_context(nc.semaphore(name))

        def need(eng, s, n):
            if not (isinstance(n, int) and n <= 0):
                eng.wait_ge(s, n)

        ident_i = sb("ident_i", [P, P], I32)
        ident = sb("ident", [P, P])
        iota_k = sb("iota_k", [P, 2 * P])
        iota_lo = sb("iota_lo", [P, HALF])
        type_id = sb("type_id", [P, 1])
        rep_i = sb("rep_i", [3 * NB, NB, D], I32)
        rep = sb("rep", [3 * NB, KT * P], BF16)
        node_id = sb("node_id", [P, SLOTS])
        pos_key = sb("pos_key", [P, P])
        eps_t = sb("eps_t", [P, 1])
        zeros = sb("zeros", [P, P], BF16)
        zrow = sb("zrow", [P, 512], BF16)
        x_sb = sb("x_sb", [P, SLOTS, D])
        src_n = sb("src_n", [BR, NBLK, P], I32)
        dst_n = sb("dst_n", [BR, NBLK, P], I32)
        typ_n = sb("typ_n", [BR, NBLK, P], I32)
        wgt_n = sb("wgt_n", [BR, NBLK, P])
        src_nf = sb("src_nf", [BR, NBLK, P])
        chunk_n = sb("chunk_n", [BR, NBLK, 2 * P])
        typ_nb = sb("typ_nb", [BR, NBLK, P], BF16)
        idx_all = sb("idx_all", [P, 2, CH], U32)
        scratch = sb("scratch", [P, 4, 2 * CH])
        n_f, row_f, slot_f, half_f = (scratch[:, i, :].rearrange("p (a c) -> p a c", a=2) for i in range(4))
        keyed = scratch[:, :, :].rearrange("p i c -> p (i c)")[:, 0:SLOTS * P].rearrange("p (s e) -> p s e", s=SLOTS)
        q_i = sb("q_i", [P, 2, CH], I32)
        k_all = sb("k_all", [P, 2, CH])
        lo_all = sb("lo_all", [P, 2, CH])
        w_all = sb("w_all", [P, CH])
        small_raw = sb("small_raw", [R, 3 * NB])
        small_res = sb("small_res", [R, 2, 3 * NB])
        small_bf = sb("small_bf", [R, 3, 3 * NB], BF16)
        rel_p = sb("rel_p", [R, 3, D], BF16)
        comp_p = sb("comp_p", [R, 3, NB], BF16)
        base_w = sb("base_w", [P, KT, D])
        a_raw = sb("a_raw", [P, 2, D])
        prod_w = sb("prod_w", [P, 4, TABW])
        bias_t = sb("bias_t", [P, 2, D])
        xT = sb("xT", [P, NT, P])
        dst_rows = sb("dst_rows", [P, SLOTS, D])
        self_rows = sb("self_rows", [P, SLOTS, D])
        stage = [sb(f"stage{i}", [P, 2, GC], U32) for i in range(2)]
        types_b = [sb(f"types_b{i}", [R, GC * P], BF16) for i in range(2)]
        type_hot = [sb(f"type_hot{i}", [R, GC * P], BF16) for i in range(2)]
        gx = [sb(f"gx{i}", [P, GC, SRCW]) for i in range(2)]
        gy = [sb(f"gy{i}", [P, GC, D]) for i in range(2)]
        compT = [sb(f"compT{i}", [3 * NB, GC * P], BF16) for i in range(2)]
        xsT = [sb(f"xsT{i}", [P, GC * P]) for i in range(2)]
        z_rows = sb("z_rows", [P, SLOTS * 2 * P])
        z = [z_rows[:, i * KT * GC * P:(i + 1) * KT * GC * P].rearrange("p (k e) -> p k e", k=KT) for i in range(2)]
        rows = z_rows[:, :].rearrange("p (s e) -> p s e", s=SLOTS)
        msgT = [sb(f"msgT{i}", [P, P]) for i in range(2)]
        yr = [sb(f"yr{i}", [P, GC, D]) for i in range(2)]
        prod = [sb(f"prod{i}", [P, GC, D]) for i in range(2)]
        score = [sb(f"score{i}", [P, GC]) for i in range(2)]
        score_r = [sb(f"score_r{i}", [P, GC]) for i in range(2)]
        att = [sb(f"att{i}", [P, GC]) for i in range(2)]
        att_lo = [sb(f"att_lo{i}", [P, GC, HALF]) for i in range(2)]
        row_hot = [sb(f"row_hot{i}", [P, GC, 2 * P]) for i in range(2)]
        spread = [sb(f"spread{i}", [P, GC, MW]) for i in range(2)]
        counts = sb("counts", [P, CH * HS])
        src_rows = counts[:, 0:SLOTS * SRCW].rearrange("p (s c) -> p s c", c=SRCW)
        before = sb("before", [P, 2, CH])
        last_f = sb("last_f", [P, SLOTS])
        last_chunk = sb("last_chunk", [P, SLOTS], U32)
        key_f = sb("key_f", [P, SLOTS])
        key_u = sb("key_u", [P, SLOTS], U32)
        last_src = sb("last_src", [P, SLOTS], U32)
        curr = sb("curr", [P, SLOTS, D])
        has_in = sb("has_in", [P, SLOTS])
        h0 = sb("h0", [P, SLOTS, D])
        h1 = sb("h1", [P, SLOTS, D])
        mean = sb("mean", [P, SLOTS])
        cen = sb("cen", [P, SLOTS, D])
        sq = sb("sq", [P, SLOTS, D])
        var = sb("var", [P, SLOTS])
        std = sb("std", [P, SLOTS])
        rstd = sb("rstd", [P, SLOTS])
        x1 = sb("x1", [P, SLOTS, LW])
        y_out = sb("y_out", [P, SLOTS, D])
        dst_stage = [sb(f"dst_stage{i}", [P, GC], U32) for i in range(2)]
        g1 = [sb(f"g1{i}", [P, GC, LW]) for i in range(2)]
        slot_hot = [sb(f"slot_hot{i}", [P, GC, HALF]) for i in range(2)]

        acc = ctx.enter_context(nc.psum_tensor("acc", [P, 2, 512], F32))
        rep_ps = ctx.enter_context(nc.psum_tensor("rep_ps", [P, 2, 512], F32))
        comp_ps = ctx.enter_context(nc.psum_tensor("comp_ps", [P, 512], F32))
        xs_ps = ctx.enter_context(nc.psum_tensor("xs_ps", [P, 512], F32))
        msgT_ps = ctx.enter_context(nc.psum_tensor("msgT_ps", [P, P], F32))
        rel_msg_ps = ctx.enter_context(nc.psum_tensor("rel_msg_ps", [P, 4, GC, D], F32))
        rel_ps, msg_ps = rel_msg_ps[:, 0:2, :, :], rel_msg_ps[:, 2:4, :, :]

        pool_const = sem("pool_const")
        dve_const = sem("dve_const")
        pads_set = sem("pads_set")
        idx_loaded = sem("idx_loaded")
        wgt_loaded = sem("wgt_loaded")
        x_loaded = sem("x_loaded")
        par_loaded = sem("par_loaded")
        small_loaded = sem("small_loaded")
        base_loaded = sem("base_loaded")
        types_stored = sem("types_stored")
        chunk_stored = sem("chunk_stored")
        src_stored = sem("src_stored")
        dst_stored = sem("dst_stored")
        self_stored = sem("self_stored")
        nat_ready = sem("nat_ready")
        typ_ready = sem("typ_ready")
        prep_pe = sem("prep_pe")
        xT_copied = sem("xT_copied")
        tab_ready = sem("tab_ready")
        idx_ready = sem("idx_ready")
        dve = sem("dve")
        parts_ready = sem("parts_ready")
        weights_ready = sem("weights_ready")
        types_loaded = [sem(f"types_loaded{i}") for i in range(2)]
        type_hot_ready = sem("type_hot_ready")
        staged = sem("staged")
        turns = sem("turns")
        gathered = [sem(f"gathered{i}") for i in range(2)]
        comp_ready = sem("comp_ready")
        comp_copied = sem("comp_copied")
        xs_ready = sem("xs_ready")
        xs_copied = sem("xs_copied")
        rel_ready = sem("rel_ready")
        rep_ready = sem("rep_ready")
        z_ready = sem("z_ready")
        msgT_ready = sem("msgT_ready")
        msgT_copied = sem("msgT_copied")
        msg_ready = sem("msg_ready")
        yr_ready = sem("yr_ready")
        prod_ready = sem("prod_ready")
        score_ready = sem("score_ready")
        relu_ready = sem("relu_ready")
        att_ready = sem("att_ready")
        lo_ready = sem("lo_ready")
        att_lo_ready = sem("att_lo_ready")
        hot_ready = sem("hot_ready")
        spread_ready = sem("spread_ready")
        scattered = sem("scattered")
        counted = sem("counted")
        last_ready = sem("last_ready")
        rows_in = [sem(f"rows_in{i}") for i in range(QS)]
        last_src_ready = sem("last_src_ready")
        curr_in = sem("curr_in")
        acc_read = sem("acc_read")
        acc_cleared = sem("acc_cleared")
        var_ready = sem("var_ready")
        std_ready = sem("std_ready")
        x1_ready = sem("x1_ready")
        x1_stored = sem("x1_stored")
        staged1 = sem("staged1")
        gathered1 = [sem(f"gathered1{i}") for i in range(2)]
        slot_ready1 = sem("slot_ready1")
        hot_ready1 = sem("hot_ready1")
        spread_ready1 = sem("spread_ready1")
        scattered1 = sem("scattered1")
        out_ready = sem("out_ready")
        out_stored = sem("out_stored")

        block = ctx.enter_context(nc.Block())

        def pairs(eng, first, last, step):
            with eng.Fori(first // 2, last // 2) as i:
                for b in range(2):
                    step(2 * i + b, b)

        def slots(eng, slot):
            slot(0, 0, 0, mid=False, old=False)
            slot(1, 1, 0, old=False)
            slot(2, 0, 1)
            slot(3, 1, 1)
            with eng.Fori(2, GROUPS // 2 - 1) as i:
                for b in range(2):
                    slot(2 * i + b, b, i)
            slot(GROUPS - 2, 0, GROUPS // 2 - 1)
            slot(GROUPS - 1, 1, GROUPS // 2 - 1, ahead=False)
            slot(GROUPS, 0, GROUPS // 2, new=False, ahead=False)
            slot(GROUPS + 1, 1, GROUPS // 2, new=False, mid=False, ahead=False)

        @block.sync
        def _(sp):
            nblk = "(b r) e -> r b e"

            def load_edges(tile, ap, s):
                full = ap[0:(NBLK - 1) * BR * P].rearrange("(b r e) -> r b e", r=BR, e=P)
                sp.dma_start(tile[:, 0:NBLK - 1, :], full).then_inc(s, 16)
                rest = ap[(NBLK - 1) * BR * P:FULL * P].rearrange("(r e) -> r e", e=P)
                sp.dma_start(tile[0:LASTROWS, NBLK - 1, :], rest).then_inc(s, 16)
                sp.dma_start(tile[LASTROWS:BR, NBLK - 1, 0:TAIL],
                             ap[FULL * P:E].rearrange("(r e) -> r e", r=1)).then_inc(s, 16)

            sp.wait_ge(pads_set, 6)
            sp.dma_start(x_sb[0:ROWS, :, :], x.rearrange("(r s) f -> r s f", s=SLOTS)).then_inc(x_loaded, 16)
            load_edges(src_n, src, idx_loaded)
            load_edges(dst_n, dst, idx_loaded)
            load_edges(typ_n, etype, idx_loaded)
            load_edges(wgt_n, weight, wgt_loaded)
            for q in range(4):
                rs = slice(q * D, (q + 1) * D)
                sp.dma_start(a_raw[rs, 0, :], a1_w).then_inc(par_loaded, 16)
                sp.dma_start(a_raw[rs, 1, :], a2_w).then_inc(par_loaded, 16)
                sp.dma_start(prod_w[rs, q, 2 * D:3 * D], self_w).then_inc(par_loaded, 16)
            sp.dma_start(bias_t[:, 0, :], a1_b.rearrange("(r f) -> r f", r=1).to_broadcast([P, D])).then_inc(par_loaded, 16)
            sp.dma_start(bias_t[:, 1, :], a2_b.rearrange("(r f) -> r f", r=1).to_broadcast([P, D])).then_inc(par_loaded, 16)
            sp.dma_start(small_raw[:, 0:D], rel_emb).then_inc(small_loaded, 16)
            sp.dma_start(small_raw[:, D:D + NB], w_comp).then_inc(small_loaded, 16)
            sp.dma_start(base_w[:, :, :], bases.rearrange("b i o -> (b i) o").rearrange("(k m) o -> m k o", k=KT)
                         ).then_inc(base_loaded, 16)
            sp.wait_ge(typ_ready, 1)
            sp.dma_start(type_tab.rearrange(nblk, b=NBLK), typ_nb[:, :, :]).then_inc(types_stored, 16)
            sp.wait_ge(tab_ready, BPT + 3 * NT)
            for tab, tile, s in ((src_tab, src_rows, src_stored), (dst_tab, dst_rows, dst_stored),
                                 (self_tab, self_rows, self_stored)):
                sp.dma_start(tab.rearrange("(r s) f -> r (s f)", s=SLOTS),
                             tile[:, :, :].rearrange("p s f -> p (s f)")).then_inc(s, 16)
            sp.wait_ge(nat_ready, 2)
            sp.dma_start(chunk_tab.rearrange(nblk, b=NBLK), chunk_n[:, :, :]).then_inc(chunk_stored, 16)

            sp.wait_ge(types_stored, 16)

            def load_types(t, b):
                need(sp, type_hot_ready, t - 1)
                sp.dma_start(types_b[b][:, :],
                             type_tab[bass.ds(t * GC, GC), :].rearrange("(a c) e -> a (c e)", a=1).to_broadcast([R, GC * P])
                             ).then_inc(types_loaded[b], 16)

            load_types(0, 0)
            load_types(1, 1)
            pairs(sp, 2, GROUPS, load_types)

            sp.wait_ge(x1_ready, 1)
            sp.dma_start(x1_tab.rearrange("(r s) f -> r (s f)", s=SLOTS),
                         x1[:, :, :].rearrange("p s f -> p (s f)")).then_inc(x1_stored, 16)
            sp.wait_ge(out_ready, 1)
            sp.dma_start(out.rearrange("(r s) f -> r (s f)", s=SLOTS),
                         y_out[0:ROWS, :, :].rearrange("p s f -> p (s f)")).then_inc(out_stored, 16)
            for s in (types_stored, chunk_stored, src_stored, dst_stored, self_stored, x1_stored, out_stored):
                sp.wait_ge(s, 16)

        @block.gpsimd
        def _(pool):
            g = nc.gpsimd
            small = dict(allow_small_or_imprecise_dtypes=True)
            g.iota(ident_i[:, :], [[1, P]], base=0, channel_multiplier=-1).then_inc(pool_const, 1)
            g.iota(rep_i[:, :, :], [[1, NB], [0, D]], base=0, channel_multiplier=-1).then_inc(pool_const, 1)
            g.iota(iota_k[:, :], [[1, 2 * P]], base=0, channel_multiplier=0, **small).then_inc(pool_const, 1)
            g.iota(iota_lo[:, :], [[1, HALF]], base=0, channel_multiplier=0, **small).then_inc(pool_const, 1)
            g.iota(type_id[:, :], [[0, 1]], base=0, channel_multiplier=1, **small).then_inc(pool_const, 1)
            g.iota(node_id[:, :], [[1, SLOTS]], base=0, channel_multiplier=SLOTS, **small).then_inc(pool_const, 1)
            g.iota(pos_key[:, :], [[KEY, P]], base=0, channel_multiplier=0, **small).then_inc(pool_const, 1)

            pool.wait_ge(src_stored, 16)
            pool.wait_ge(dst_stored, 16)
            pool.wait_ge(idx_ready, 1)

            def gather_group(t, b, done):
                need(pool, gathered[b], done)
                g.tensor_copy(stage[b][:, :, :], idx_all[:, :, bass.ds(t * GC, GC)]).then_inc(staged, 1)
                need(pool, prod_ready, t - 1)
                need(pool, xs_ready, t - 1)
                pool.wait_ge(staged, t + 1)
                pool.sem_inc(turns, 1)
                for j in range(GC):
                    g.indirect_dma_start(gx[b][:, j, :], None, src_tab,
                                         bass.IndirectOffsetOnAxis(stage[b][:, 0, j:j + 1], 0)).then_inc(gathered[b], 16)
                    g.indirect_dma_start(gy[b][:, j, :], None, dst_tab,
                                         bass.IndirectOffsetOnAxis(stage[b][:, 1, j:j + 1], 0)).then_inc(gathered[b], 16)

            gather_group(0, 0, 0)
            gather_group(1, 1, 0)
            with pool.Fori(1, GROUPS // 2) as i:
                for b in range(2):
                    gather_group(2 * i + b, b, i * (32 * GC))

            pool.wait_ge(chunk_stored, 16)
            pool.wait_ge(self_stored, 16)
            pool.wait_ge(last_ready, 1)
            for s in range(SLOTS):
                g.indirect_dma_start(rows[:, s, :], None, chunk_tab,
                                     bass.IndirectOffsetOnAxis(last_chunk[:, s:s + 1], 0)).then_inc(rows_in[s // SQ], 16)
            for s in range(SLOTS):
                if s % SQ == 0:
                    pool.wait_ge(last_src_ready, s // SQ + 1)
                g.indirect_dma_start(curr[:, s, :], None, self_tab,
                                     bass.IndirectOffsetOnAxis(last_src[:, s:s + 1], 0)).then_inc(curr_in, 16)

            pool.wait_ge(x1_stored, 16)

            def gather_group1(t, b, done):
                need(pool, gathered1[b], done)
                g.tensor_copy(dst_stage[b][:, :], idx_all[:, 1, bass.ds(t * GC, GC)]).then_inc(staged1, 1)
                need(pool, spread_ready1, (t - 1) * GC)
                pool.wait_ge(staged1, t + 1)
                pool.sem_inc(turns, 1)
                for j in range(GC):
                    g.indirect_dma_start(g1[b][:, j, :], None, x1_tab,
                                         bass.IndirectOffsetOnAxis(dst_stage[b][:, j:j + 1], 0)).then_inc(gathered1[b], 16)

            gather_group1(0, 0, 0)
            gather_group1(1, 1, 0)
            with pool.Fori(1, GROUPS // 2) as i:
                for b in range(2):
                    gather_group1(2 * i + b, b, i * (16 * GC))

        @block.tensor
        def _(pe):
            te = nc.tensor
            pe.wait_ge(dve_const, 1)
            pe.wait_ge(nat_ready, 2)
            pe.wait_ge(wgt_loaded, 48)
            for ps, tile in ((acc[:, 0, :], src_nf[:, :, :]), (acc[:, 1, :], chunk_n[:, :, 0:P]),
                             (comp_ps[:, :], wgt_n[:, :, :])):
                for b in range(NBLK):
                    m = te.transpose(ps[:, b * BR:(b + 1) * BR], tile[:, b, :], ident[0:BR, 0:BR])
                m.then_inc(prep_pe, 1)
            pe.wait_ge(x_loaded, 16)
            pe.wait_ge(weights_ready, 1)
            for j in range(NT):
                ns = min(4, SLOTS - 4 * j)
                if j >= 2:
                    pe.wait_ge(xT_copied, j - 1)
                te.transpose(xs_ps[0:ns * D, (j % 2) * P:(j % 2) * P + P],
                             x_sb[:, 4 * j:4 * j + ns, :].rearrange("p s f -> p (s f)"), ident[:, :]
                             ).then_inc(prep_pe, 1)
                pe.wait_ge(xT_copied, j + 1)
                if j >= 2:
                    pe.wait_ge(tab_ready, BPT + 3 * (j - 1))
                te.matmul(rep_ps[:, j % 2, 0:ns * TABW], xT[0:ns * D, j, :],
                          prod_w[0:ns * D, 0:ns, :].rearrange("p s c -> p (s c)"),
                          start=True, stop=True).then_inc(prep_pe, 1)
            pe.wait_ge(idx_ready, 1)
            for h in range(2):
                m = te.matmul(acc[:, h, 0:MW], zeros[:, :], zrow[:, 0:MW], start=True, stop=True)
            m.then_inc(acc_cleared, 1)
            pe.wait_ge(tab_ready, BPT + 3 * NT)
            pe.wait_ge(parts_ready, 1)
            pe.wait_ge(base_loaded, 16)

            def look_up_comp(t, b):
                pe.wait_ge(type_hot_ready, t + 1)
                need(pe, comp_copied, t)
                te.matmul(comp_ps[0:3 * NB, :], comp_p[:, :, :].rearrange("r a c -> r (a c)"), type_hot[b][:, :],
                          start=True, stop=True).then_inc(comp_ready, 1)

            def turn_x(t, b, chunks, got):
                if chunks[0] == 0:
                    need(pe, xs_copied, t)
                    pe.wait_ge(gathered[b], got)
                for j in chunks:
                    m = te.transpose(xs_ps[:, j * P:(j + 1) * P], gx[b][:, j, 0:P], ident[:, :])
                if chunks[-1] == GC - 1:
                    m.then_inc(xs_ready, 1)

            def look_up_rel(t, b):
                need(pe, yr_ready, t)
                for j in range(GC):
                    for a in range(3):
                        m = te.matmul(rel_ps[:, b, j, :], type_hot[b][:, j * P:(j + 1) * P], rel_p[:, a, :],
                                      start=(a == 0), stop=(a == 2))
                m.then_inc(rel_ready, 1)

            def repeat_comp(t, b, k):
                if k == 0:
                    pe.wait_ge(comp_copied, t + 1)
                need(pe, z_ready, t * KT + k - 1)
                te.matmul(rep_ps[:, k % 2, :], rep[:, k * P:(k + 1) * P], compT[b][:, :],
                          start=True, stop=True).then_inc(rep_ready, 1)

            def scatter(t, b, j):
                if j == 0:
                    pe.wait_ge(hot_ready, t + 1)
                pe.wait_ge(spread_ready, t * GC + j + 1)
                need(pe, counted, t * GC + j)
                for h in range(2):
                    m = te.matmul(acc[:, h, 0:MW], row_hot[b][:, j, h * P:(h + 1) * P], spread[b][:, j, :],
                                  start=False, stop=True, skip_group_check=True)
                m.then_inc(scattered, 1)

            def messages(t, b, k):
                if k == 0:
                    pe.wait_ge(z_ready, (t + 1) * KT)
                    need(pe, msgT_copied, t)
                for j in range(GC):
                    m = te.matmul(msgT_ps[j * D:(j + 1) * D, :], base_w[:, k, :], z[b][:, k, j * P:(j + 1) * P],
                                  start=(k == 0), stop=(k == KT - 1))
                if k == KT - 1:
                    m.then_inc(msgT_ready, 1)

            def turn_messages(t, b):
                pe.wait_ge(msgT_copied, t + 1)
                te.transpose(msg_ps[:, b, :, :].rearrange("p c f -> p (c f)"), msgT[b][:, :], ident[:, :]
                             ).then_inc(msg_ready, 1)

            def slot(t, b, half, new=True, mid=True, old=True, ahead=True):
                got = (half + 1 if b == 0 else half + 2) * (32 * GC)
                for j in range(GC):
                    if new:
                        repeat_comp(t, b, j)
                    if mid:
                        messages(t - 1, 1 - b, j)
                    if ahead and j == 1:
                        look_up_comp(t + 1, 1 - b)
                    if ahead and j >= 2:
                        turn_x(t + 1, 1 - b, (0, 1) if j == 2 else (2, 3), got)
                    if old:
                        scatter(t - 2, b, j)
                if ahead:
                    look_up_rel(t + 1, 1 - b)
                if mid:
                    turn_messages(t - 1, 1 - b)

            look_up_comp(0, 0)
            turn_x(0, 0, range(GC), 32 * GC)
            look_up_rel(0, 0)
            slots(pe, slot)

            pe.wait_ge(acc_read, 1)
            pe.wait_ge(counted, CH)
            for h in range(2):
                m = te.matmul(acc[:, h, 0:MW], zeros[:, :], zrow[:, 0:MW], start=True, stop=True)
            m.then_inc(acc_cleared, 1)

            def scatter1(t, b):
                pe.wait_ge(hot_ready1, t + 1)
                for j in range(GC):
                    pe.wait_ge(spread_ready1, t * GC + (j + 1))
                    for h in range(2):
                        m = te.matmul(acc[:, h, 0:MW], row_hot[b][:, j, h * P:(h + 1) * P], spread[b][:, j, :],
                                      start=False, stop=True, skip_group_check=True)
                    m.then_inc(scattered1, 1)

            with pe.Fori(0, GROUPS // 2) as i:
                for b in range(2):
                    scatter1(2 * i + b, b)

        @block.scalar
        def _(act):
            sc = nc.scalar

            def copy_comp(t, b):
                act.wait_ge(comp_ready, t + 1)
                need(act, rep_ready, (t - 1) * KT)
                sc.activation(compT[b][:, :], comp_ps[0:3 * NB, :], ACT.Copy).then_inc(comp_copied, 1)

            def copy_xs(t, b):
                act.wait_ge(xs_ready, t + 1)
                need(act, z_ready, (t - 1) * KT)
                sc.activation(xsT[b][:, :], xs_ps[:, :], ACT.Copy).then_inc(xs_copied, 1)

            def count(t, j):
                c = t * GC + j
                act.wait_ge(scattered, c + 1)
                sc.activation(counts[:, bass.ds(c * HS, HS)].rearrange("p (h l) -> p h l", h=2),
                              acc[:, :, VW:MW], ACT.Copy).then_inc(counted, 1)

            def attention(t, b):
                act.wait_ge(score_ready, t + 1)
                sc.activation(score_r[b][:, :], score[b][:, :], ACT.Relu, scale=float(D) ** -0.5).then_inc(relu_ready, 1)
                act.wait_ge(relu_ready, t + 1)
                need(act, att_lo_ready, t - 1)
                sc.activation(att[b][:, :], score_r[b][:, :], ACT.Tanh).then_inc(att_ready, 1)

            def slot(t, b, half, new=True, mid=True, old=True, ahead=True):
                if old:
                    count(t - 2, 0)
                    count(t - 2, 1)
                if new:
                    attention(t, b)
                if ahead:
                    copy_comp(t + 1, 1 - b)
                if old:
                    count(t - 2, 2)
                if mid:
                    act.wait_ge(msgT_ready, t)
                    need(act, msg_ready, t - 2)
                    sc.activation(msgT[1 - b][:, :], msgT_ps[:, :], ACT.Copy).then_inc(msgT_copied, 1)
                if ahead:
                    copy_xs(t + 1, 1 - b)
                if old:
                    count(t - 2, 3)

            copy_comp(0, 0)
            copy_xs(0, 0)
            slots(act, slot)
            for n in range(2):
                act.wait_ge(var_ready, n + 1)
                sc.activation(std[:, :], var[:, :], ACT.Sqrt, bias=eps_t[:, 0:1], scale=1.0 / D).then_inc(std_ready, 1)

        @block.vector
        def _(ve):
            v = nc.vector
            done = [0]

            def link(ins):
                done[0] += 1
                ins.then_inc(dve, 1)
                ve.wait_ge(dve, done[0])

            def slots_b(ap, n=D):
                return ap.unsqueeze(2).to_broadcast([P, ap.shape[1], n])

            v.memset(src_n[:, NBLK - 1, :], PAD).then_inc(pads_set, 1)
            v.memset(dst_n[:, NBLK - 1, :], PAD).then_inc(pads_set, 1)
            v.memset(typ_n[:, NBLK - 1, :], 0).then_inc(pads_set, 1)
            v.memset(wgt_n[:, NBLK - 1, :], 0.0).then_inc(pads_set, 1)
            v.memset(x_sb[96:P, :, :], 0.0).then_inc(pads_set, 1)
            v.memset(zeros[:, :], 0.0)
            v.memset(zrow[:, :], 0.0)
            v.memset(eps_t[:, :], EPS)
            v.memset(x1[:, :, D:LW], 1.0)
            v.memset(prod_w[:, :, :], 0.0).then_inc(pads_set, 1)
            ve.wait_ge(pool_const, 7)
            v.tensor_scalar(ident[:, :], ident_i[:, :], 0.0, None, ALU.is_equal).then_inc(dve_const, 1)
            link(v.tensor_scalar(rep_i[:, :, :], rep_i[:, :, :], NB - 1, None, ALU.bitwise_and))
            link(v.tensor_scalar(rep[:, :], rep_i[:, :, :].rearrange("p b f -> p (b f)"), 0.0, None, ALU.is_equal))
            ve.wait_ge(idx_loaded, 3 * 48)
            v.tensor_copy(typ_nb[:, :, :], typ_n[:, :, :]).then_inc(typ_ready, 1)
            v.tensor_copy(chunk_n[:, :, 0:P], dst_n[:, :, :]).then_inc(nat_ready, 1)
            link(v.tensor_copy(src_nf[:, :, :], src_n[:, :, :]))
            v.tensor_tensor(chunk_n[:, :, P:2 * P], src_nf[:, :, :],
                            pos_key[0:BR, :].unsqueeze(1).to_broadcast([BR, NBLK, P]), ALU.add).then_inc(nat_ready, 1)
            ve.wait_ge(par_loaded, 14 * 16)
            for q in range(4):
                rs = slice(q * D, (q + 1) * D)
                v.transpose(prod_w[rs, q, 0:D], a_raw[rs, 0, :])
                m = v.transpose(prod_w[rs, q, D:2 * D], a_raw[rs, 1, :])
            m.then_inc(weights_ready, 1)
            ve.wait_ge(x_loaded, 16)
            for r in range(BPT):
                v.tensor_copy(src_rows[:, :, r * D:(r + 1) * D], x_sb[:, :, :]).then_inc(tab_ready, 1)
            for j in range(NT):
                ns = min(4, SLOTS - 4 * j)
                s = slice(4 * j, 4 * j + ns)
                ve.wait_ge(prep_pe, 4 + 2 * j)
                v.tensor_copy(xT[0:ns * D, j, :], xs_ps[0:ns * D, (j % 2) * P:(j % 2) * P + P]).then_inc(xT_copied, 1)
                ve.wait_ge(prep_pe, 5 + 2 * j)
                got = rep_ps[:, j % 2, 0:ns * TABW].rearrange("p (s c) -> p s c", c=TABW)
                bias = [bias_t[:, a, :].unsqueeze(1).to_broadcast([P, ns, D]) for a in range(2)]
                v.tensor_tensor(src_rows[:, s, P:SRCW], got[:, :, 0:D], bias[0], ALU.add).then_inc(tab_ready, 1)
                v.tensor_tensor(dst_rows[:, s, :], got[:, :, D:2 * D], bias[1], ALU.add).then_inc(tab_ready, 1)
                v.tensor_copy(self_rows[:, s, :], got[:, :, 2 * D:3 * D]).then_inc(tab_ready, 1)
            ve.wait_ge(prep_pe, 3)
            for a in range(2):
                v.tensor_copy(idx_all[:, a, :], acc[:, a, 0:CH])
                link(v.tensor_copy(n_f[:, a, :], acc[:, a, 0:CH]))
            v.tensor_copy(w_all[:, :], comp_ps[:, 0:CH])
            link(v.tensor_scalar(q_i[:, :, :], n_f[:, :, :], float(RECIP), None, ALU.mult))
            link(v.tensor_scalar(q_i[:, :, :], q_i[:, :, :], SHIFT, None, ALU.logical_shift_right))
            link(v.tensor_copy(row_f[:, :, :], q_i[:, :, :]))
            link(v.scalar_tensor_tensor(slot_f[:, :, :], row_f[:, :, :], -float(SLOTS), n_f[:, :, :], ALU.mult, ALU.add))
            link(v.tensor_scalar(half_f[:, :, :], slot_f[:, :, :], float(HALF), None, ALU.is_ge))
            link(v.scalar_tensor_tensor(k_all[:, :, :], half_f[:, :, :], float(P), row_f[:, :, :], ALU.mult, ALU.add))
            link(v.scalar_tensor_tensor(lo_all[:, :, :], half_f[:, :, :], -float(HALF), slot_f[:, :, :],
                                        ALU.mult, ALU.add))
            v.memset(has_in[:, :], 0.0).then_inc(idx_ready, 1)
            ve.wait_ge(small_loaded, 32)
            link(v.tensor_copy(small_bf[:, 0, :], small_raw[:, :]))
            link(v.tensor_tensor(small_res[:, 0, :], small_raw[:, :], small_bf[:, 0, :], ALU.subtract))
            link(v.tensor_copy(small_bf[:, 1, :], small_res[:, 0, :]))
            link(v.tensor_tensor(small_res[:, 1, :], small_res[:, 0, :], small_bf[:, 1, :], ALU.subtract))
            link(v.tensor_copy(small_bf[:, 2, :], small_res[:, 1, :]))
            v.tensor_copy(rel_p[:, :, :], small_bf[:, :, 0:D])
            link(v.tensor_copy(comp_p[:, :, :], small_bf[:, :, D:D + NB]))
            v.memset(last_f[:, :], 0.0).then_inc(parts_ready, 1)

            def type_one_hot(t, b, got):
                ve.wait_ge(types_loaded[b], got)
                need(ve, rel_ready, t - 1)
                v.tensor_scalar(type_hot[b][:, :], types_b[b][:, :], type_id[0:R, 0:1], None,
                                ALU.is_equal).then_inc(type_hot_ready, 1)

            def times_x(t, b, k):
                ve.wait_ge(rep_ready, t * KT + (k + 1))
                if k == 0:
                    ve.wait_ge(xs_copied, t + 1)
                    need(ve, msgT_ready, t - 1)
                v.tensor_tensor(z[b][:, k, :], rep_ps[:, k % 2, :], xsT[b][:, :], ALU.mult).then_inc(z_ready, 1)

            def one_hots(t, b, a, hot, lo, hot_sem, lo_sem):
                c = bass.ds(t * GC, GC)
                v.tensor_tensor(lo, iota_lo[:, :].unsqueeze(1).to_broadcast([P, GC, HALF]),
                                lo_all[:, a, c].unsqueeze(2).to_broadcast([P, GC, HALF]),
                                ALU.is_equal).then_inc(lo_sem, 1)
                v.tensor_tensor(hot, iota_k[:, :].unsqueeze(1).to_broadcast([P, GC, 2 * P]),
                                k_all[:, a, c].unsqueeze(2).to_broadcast([P, GC, 2 * P]),
                                ALU.is_equal).then_inc(hot_sem, 1)

            def spread_msg(t, b, j):
                if j == 0:
                    ve.wait_ge(msg_ready, t + 1)
                    ve.wait_ge(att_lo_ready, t + 1)
                v.tensor_tensor(spread[b][:, j, 0:VW].rearrange("p (l f) -> p l f", f=D),
                                att_lo[b][:, j, :].unsqueeze(2).to_broadcast([P, HALF, D]),
                                msg_ps[:, b, j, :].unsqueeze(1).to_broadcast([P, HALF, D]),
                                ALU.mult).then_inc(spread_ready, 1)

            def slot(t, b, half, new=True, mid=True, old=True, ahead=True):
                if old:
                    spread_msg(t - 2, b, 0)
                if new:
                    times_x(t, b, 0)
                    ve.wait_ge(rel_ready, t + 1)
                    ve.wait_ge(gathered[b], (half + 1) * (32 * GC))
                    v.tensor_tensor(yr[b][:, :, :], rel_ps[:, b, :, :], gy[b][:, :, :], ALU.add).then_inc(yr_ready, 1)
                if ahead:
                    type_one_hot(t + 1, 1 - b, (half + 1 if b == 1 else half) * 16 + 16)
                if old:
                    spread_msg(t - 2, b, 1)
                if new:
                    ve.wait_ge(yr_ready, t + 1)
                    v.tensor_tensor(prod[b][:, :, :], yr[b][:, :, :], gx[b][:, :, P:SRCW], ALU.mult
                                    ).then_inc(prod_ready, 1)
                    times_x(t, b, 1)
                    ve.wait_ge(prod_ready, t + 1)
                    need(ve, relu_ready, t - 1)
                    v.tensor_reduce(score[b][:, :], prod[b][:, :, :], AX, ALU.add).then_inc(score_ready, 1)
                if old:
                    spread_msg(t - 2, b, 2)
                if new:
                    times_x(t, b, 2)
                if old:
                    spread_msg(t - 2, b, 3)
                if new:
                    times_x(t, b, 3)
                if mid:
                    u, c = t - 1, 1 - b
                    need(ve, scattered, (u - 1) * GC)
                    one_hots(u, c, 1, row_hot[c][:, :, :], spread[c][:, :, VW:MW], hot_ready, lo_ready)
                    ve.wait_ge(att_ready, u + 1)
                    ve.wait_ge(lo_ready, u + 1)
                    v.tensor_tensor(att_lo[c][:, :, :], spread[c][:, :, VW:MW],
                                    att[c][:, :].unsqueeze(2).to_broadcast([P, GC, HALF]), ALU.mult
                                    ).then_inc(att_lo_ready, 1)

            type_one_hot(0, 0, 16)
            slots(ve, slot)

            ve.wait_ge(counted, CH)
            cnt = counts[:, :].rearrange("p (c s) -> p s c", s=HS)
            for s in range(SLOTS):
                link(v.tensor_scalar(before[:, s % 2, :], cnt[:, s, :], counts[:, (CH - 1) * HS + s:(CH - 1) * HS + s + 1],
                                     0.0, ALU.is_lt, ALU.add, accum_out=last_f[:, s:s + 1]))
            v.tensor_copy(last_chunk[:, :], last_f[:, :]).then_inc(last_ready, 1)
            ve.wait_ge(scattered, CH)
            v.tensor_scalar(has_in[:, :], counts[:, (CH - 1) * HS:(CH - 1) * HS + SLOTS], 0.0, None, ALU.is_gt)
            v.tensor_copy(h0[:, 0:HALF, :], acc[:, 0, 0:VW].rearrange("p (l f) -> p l f", f=D))
            link(v.tensor_copy(h0[:, HALF:SLOTS, :],
                               acc[:, 1, 0:(SLOTS - HALF) * D].rearrange("p (l f) -> p l f", f=D)))
            v.memset(score[0][:, :], 0.0).then_inc(acc_read, 1)
            for q in range(QS):
                ss = slice(q * SQ, (q + 1) * SQ)
                ve.wait_ge(rows_in[q], 16 * SQ)
                for s in range(q * SQ, (q + 1) * SQ):
                    m = v.scalar_tensor_tensor(keyed[:, s, :], rows[:, s, 0:P], node_id[:, s:s + 1], rows[:, s, P:2 * P],
                                               ALU.is_equal, ALU.mult)
                link(m)
                link(v.tensor_reduce(key_f[:, ss], keyed[:, ss, :], AX, ALU.max))
                link(v.tensor_copy(key_u[:, ss], key_f[:, ss]))
                v.tensor_scalar(last_src[:, ss], key_u[:, ss], KEY - 1, None, ALU.bitwise_and).then_inc(last_src_ready, 1)

            def layer_norm(h, o, n):
                link(v.tensor_reduce(mean[:, :], h[:, :, :], AX, ALU.add))
                link(v.tensor_scalar(mean[:, :], mean[:, :], 1.0 / D, None, ALU.mult))
                link(v.tensor_tensor(cen[:, :, :], h[:, :, :], slots_b(mean[:, :]), ALU.subtract))
                link(v.tensor_tensor(sq[:, :, :], cen[:, :, :], cen[:, :, :], ALU.mult))
                v.tensor_reduce(var[:, :], sq[:, :, :], AX, ALU.add).then_inc(var_ready, 1)
                ve.wait_ge(std_ready, n)
                link(v.reciprocal(rstd[:, :], std[:, :]))
                link(v.tensor_tensor(o, cen[:, :, :], slots_b(rstd[:, :]), ALU.mult))

            ve.wait_ge(curr_in, 16 * SLOTS)
            link(v.tensor_tensor(h1[:, :, :], h0[:, :, :], curr[:, :, :], ALU.add))
            link(v.scalar_tensor_tensor(h0[:, :, :], h1[:, :, :], 0.0, slots_b(has_in[:, :]), ALU.max, ALU.mult))
            link(v.tensor_tensor(h1[:, :, :], h0[:, :, :], x_sb[:, :, :], ALU.add))
            layer_norm(h1, x1[:, :, 0:D], 1)
            v.memset(score[0][:, :], 0.0).then_inc(x1_ready, 1)

            def spread1(t, b, got, reuse):
                if reuse:
                    ve.wait_ge(scattered1, (t - 1) * GC)
                c = bass.ds(t * GC, GC)
                one_hots(t, b, 0, row_hot[b][:, :, :], slot_hot[b][:, :, :], hot_ready1, slot_ready1)
                ve.wait_ge(slot_ready1, t + 1)
                v.tensor_tensor(att_lo[b][:, :, :], slot_hot[b][:, :, :],
                                w_all[:, c].unsqueeze(2).to_broadcast([P, GC, HALF]), ALU.mult).then_inc(att_lo_ready, 1)
                ve.wait_ge(att_lo_ready, t + (GROUPS + 1))
                ve.wait_ge(gathered1[b], got)
                for j in range(GC):
                    v.tensor_tensor(spread[b][:, j, :].rearrange("p (l f) -> p l f", f=LW),
                                    att_lo[b][:, j, :].unsqueeze(2).to_broadcast([P, HALF, LW]),
                                    g1[b][:, j, :].unsqueeze(1).to_broadcast([P, HALF, LW]),
                                    ALU.mult).then_inc(spread_ready1, 1)

            spread1(0, 0, 16 * GC, False)
            spread1(1, 1, 16 * GC, False)
            with ve.Fori(1, GROUPS // 2) as i:
                for b in range(2):
                    spread1(2 * i + b, b, (i + 1) * (16 * GC), True)

            ve.wait_ge(scattered1, CH)
            for h, n in ((0, HALF), (1, SLOTS - HALF)):
                part = acc[:, h, 0:n * LW].rearrange("p (l f) -> p l f", f=LW)
                ss = slice(h * HALF, h * HALF + n)
                v.tensor_tensor(h0[:, ss, :], part[:, :, 0:D], x1[:, ss, 0:D], ALU.add)
                link(v.tensor_tensor(h1[:, ss, :], x1[:, ss, 0:D], part[:, :, D:LW].to_broadcast([P, n, D]), ALU.mult))
            link(v.tensor_tensor(h0[:, :, :], h0[:, :, :], h1[:, :, :], ALU.subtract))
            layer_norm(h0, y_out[:, :, :], 2)
            v.memset(score[0][:, :], 0.0).then_inc(out_ready, 1)


_INS = ["x", "src", "dst", "edge_type_86", "edge_weight", "L0_gnn_weight", "L0_gnn_w_comp", "L0_gnn_self_loop_weight",
        "L0_gnn_A1_w", "L0_gnn_A1_b", "L0_gnn_A2_w", "L0_gnn_A2_b", "L0_gnn_rel_emb"]


def kernel(**inputs):
    import numpy as _np
    import concourse.bacc as _bacc
    from concourse import mybir as _mybir
    from concourse.bass_utils import run_bass_kernel_spmd as _run

    nc = _bacc.Bacc("TRN2", target_bir_lowering=False, num_devices=1)
    arrays, args = {}, []
    for name in _INS:
        a = _np.ascontiguousarray(inputs[name])
        arrays[f"in_{name}_dram"] = a
        args.append(nc.dram_tensor(f"in_{name}_dram", a.shape, _mybir.dt.from_np(a.dtype), kind="ExternalInput").ap())
    shape = tuple(inputs["x"].shape)
    out = nc.dram_tensor("out_0_dram", shape, _mybir.dt.float32, kind="ExternalOutput").ap()
    graph_kernel(nc, *args, out)
    r = _run(nc, [arrays], core_ids=[0])
    return r.results[0]["out_0_dram"]
```

```python
from collections import namedtuple
from contextlib import ExitStack

import numpy as np

import concourse.bass as bass
import concourse.mybir as mybir
from concourse.alu_op_type import AluOpType as ALU

F32 = mybir.dt.float32
BF16 = mybir.dt.bfloat16
I32 = mybir.dt.int32
U32 = mybir.dt.uint32
ACT = mybir.ActivationFunctionType
AX = mybir.AxisListType.X

P = 128
D = 32
NB = 16
EPS = 1e-5
SLOTS = 25
PARTS = (8, 7, 10)
WIDE = max(PARTS)
LEFT = PARTS[0] + PARTS[1]
BANKS = (slice(0, LEFT), slice(LEFT, SLOTS))
GC = 4
KT = NB * D // P
BPT = P // D
KEY = 4096
RECIP, SHIFT = 5243, 17
LW = D + 2
MW = WIDE * LW
TERMS = 3
SRCW = P + D
TABW = 3 * D


There = namedtuple("There", "ahead new turn weigh spread count")


def graph_kernel(nc, x, src, dst, etype, weight, bases, w_comp, self_w, a1_w, a1_b, a2_w, a2_b, rel_emb, out):
    N, E, R = x.shape[0], src.shape[0], w_comp.shape[0]
    ROWS = N // SLOTS
    PAD = N
    assert N == ROWS * SLOTS and ROWS < P
    CH = -(-E // (P * GC)) * GC
    GROUPS = CH // GC
    NBLK = 4
    BR = CH // NBLK
    FULL = E // P
    TAIL = E - FULL * P
    LASTROWS = FULL - (NBLK - 1) * BR
    assert CH == BR * NBLK and LASTROWS == BR - 1 and GROUPS % 4 == 0
    NT = -(-SLOTS // 4)
    TAB_CUTS = (0, 3, 5, NT)
    PIECES = len(TAB_CUTS) - 1
    SQ = 5
    QS = SLOTS // SQ
    TG = 5
    TC = TG * GC
    TB = 4
    assert TC % TB == 0 and TC * WIDE <= MW and TC * SLOTS <= 512 and TB // 2 * (TC // TB) * 3 * P <= GC * TERMS * MW

    src_tab = nc.dram_tensor("src_tab", [P * SLOTS, SRCW], F32).ap()
    dst_tab = nc.dram_tensor("dst_tab", [P * SLOTS, D], F32).ap()
    self_tab = nc.dram_tensor("self_tab", [P * SLOTS, D], F32).ap()
    x1_tab = nc.dram_tensor("x1_tab", [P * SLOTS, LW], F32).ap()
    chunk_tab = nc.dram_tensor("chunk_tab", [CH, 2 * P], F32).ap()
    type_tab = nc.dram_tensor("type_tab", [CH, P], BF16).ap()

    ctx = ExitStack()
    with ctx:
        def sb(name, shape, dt=F32):
            return ctx.enter_context(nc.sbuf_tensor(name, shape, dt))

        def sem(name):
            return ctx.enter_context(nc.semaphore(name))

        def need(eng, s, n):
            if not (isinstance(n, int) and n <= 0):
                eng.wait_ge(s, n)

        ident_i = sb("ident_i", [P, P], I32)
        ident = sb("ident", [P, P])
        iota_k = sb("iota_k", [P, 3 * P])
        type_id = sb("type_id", [P, 1])
        rep_i = sb("rep_i", [3 * NB, NB, D], I32)
        rep = sb("rep", [3 * NB, KT * P], BF16)
        node_id = sb("node_id", [P, SLOTS])
        pos_key = sb("pos_key", [P, P])
        eps_t = sb("eps_t", [P, 1])
        iota_lx = sb("iota_lx", [P, WIDE, LW], BF16)
        ones = sb("ones", [P, 1])
        neg_k = sb("neg_k", [P, 2, CH])
        zeros = sb("zeros", [P, P], BF16)
        zrow = sb("zrow", [P, 512], BF16)
        x_sb = sb("x_sb", [P, SLOTS, D])
        src_n = sb("src_n", [BR, NBLK, P], I32)
        dst_n = sb("dst_n", [BR, NBLK, P], I32)
        typ_n = sb("typ_n", [BR, NBLK, P], I32)
        wgt_n = sb("wgt_n", [BR, NBLK, P])
        src_nf = sb("src_nf", [BR, NBLK, P])
        chunk_n = sb("chunk_n", [BR, NBLK, 2 * P])
        typ_nb = sb("typ_nb", [BR, NBLK, P], BF16)
        idx_all = sb("idx_all", [P, 2, CH], U32)
        scratch = sb("scratch", [P, 4, 2 * CH])
        n_f, row_f, slot_f, part_f = (scratch[:, i, :].rearrange("p (a c) -> p a c", a=2) for i in range(4))
        keyed = scratch[:, :, :].rearrange("p i c -> p (i c)")[:, 0:SLOTS * P].rearrange("p (s e) -> p s e", s=SLOTS)
        q_i = sb("q_i", [P, 2, CH], I32)
        k_all = sb("k_all", [P, 2, CH])
        lo_all = sb("lo_all", [P, 2, CH])
        w_all = sb("w_all", [P, CH])
        small_raw = sb("small_raw", [R, 3 * NB])
        small_res = sb("small_res", [R, 2, 3 * NB])
        small_bf = sb("small_bf", [R, 3, 3 * NB], BF16)
        rel_p = sb("rel_p", [R, 3, D], BF16)
        comp_p = sb("comp_p", [R, 3, NB], BF16)
        base_w = sb("base_w", [P, KT, D])
        w_raw = sb("w_raw", [D, 3, D])
        prod_w = sb("prod_w", [P, 4, TABW])
        bias_t = sb("bias_t", [P, 2, D])
        xT = sb("xT", [P, NT, P])
        dst_rows = sb("dst_rows", [P, SLOTS, D])
        self_rows = sb("self_rows", [P, SLOTS, D])
        stage = [sb(f"stage{i}", [P, 2, 2 * GC], U32) for i in range(2)]
        types_b = [sb(f"types_b{i}", [R, GC * P], BF16) for i in range(2)]
        type_hot = [sb(f"type_hot{i}", [R, GC * P], BF16) for i in range(2)]
        gx = [sb(f"gx{i}", [P, GC, SRCW]) for i in range(2)]
        gy = [sb(f"gy{i}", [P, GC, D]) for i in range(2)]
        compT = [sb(f"compT{i}", [3 * NB, GC * P], BF16) for i in range(2)]
        xsT = [sb(f"xsT{i}", [P, GC * P]) for i in range(2)]
        z = [sb(f"z{i}", [P, KT, GC * P]) for i in range(2)]
        msgT = [sb(f"msgT{i}", [P, P]) for i in range(2)]
        yr = [sb(f"yr{i}", [P, GC, D]) for i in range(2)]
        prod = [sb(f"prod{i}", [P, GC, D]) for i in range(2)]
        score = [sb(f"score{i}", [P, GC]) for i in range(2)]
        score_r = [sb(f"score_r{i}", [P, GC]) for i in range(2)]
        att = [sb(f"att{i}", [P, GC]) for i in range(2)]
        row_hot = [sb(f"row_hot{i}", [P, GC, 3 * P], BF16) for i in range(2)]
        slot_hot = [sb(f"slot_hot{i}", [P, GC, MW], BF16) for i in range(2)]
        spread = [sb(f"spread{i}", [P, GC, TERMS, MW], BF16) for i in range(2)]
        wx = [sb(f"wx{i}", [P, GC, LW]) for i in range(2)]
        wx_rest = [sb(f"wx_rest{i}", [P, GC, LW]) for i in range(2)]
        wx_terms = [sb(f"wx_terms{i}", [P, GC, TERMS, LW], BF16) for i in range(2)]
        counts = sb("counts", [P, (CH + 1) * SLOTS])
        rows = counts[:, 0:SLOTS * 2 * P].rearrange("p (s e) -> p s e", s=SLOTS)
        assert SLOTS * 2 * P <= (CH - TC) * SLOTS
        src_rows = counts[:, 0:SLOTS * SRCW].rearrange("p (s c) -> p s c", c=SRCW)
        chunk_no = sb("chunk_no", [P, CH])
        grew = [sb(f"grew{i}", [P, GC, SLOTS]) for i in range(2)]
        grew_at = [sb(f"grew_at{i}", [P, GC, SLOTS]) for i in range(2)]
        last_of = sb("last_of", [P, GC, SLOTS])
        tail_last = sb("tail_last", [P, SLOTS])
        tail_hot = [spread[q // 2][:, :, :, :].rearrange("p c a m -> p (c a m)")
                    [:, (q % 2) * (TC // TB) * 3 * P:(q % 2 + 1) * (TC // TB) * 3 * P]
                    .rearrange("p (c k) -> p c k", k=3 * P) for q in range(TB)]
        tail_slot_hot = slot_hot[0][:, 0, 0:TC * WIDE].rearrange("p (c l) -> p c l", l=WIDE)
        tail_grew, tail_at = (scratch[:, i, 0:TC * SLOTS].rearrange("p (c s) -> p c s", s=SLOTS) for i in range(2))
        last_f = sb("last_f", [P, SLOTS])
        last_chunk = sb("last_chunk", [P, SLOTS], U32)
        key_f = sb("key_f", [P, SLOTS])
        key_u = sb("key_u", [P, SLOTS], U32)
        last_src = sb("last_src", [P, SLOTS], U32)
        curr = sb("curr", [P, SLOTS, D])
        has_in = sb("has_in", [P, SLOTS])
        h0 = sb("h0", [P, SLOTS, D])
        h1 = sb("h1", [P, SLOTS, D])
        mean = sb("mean", [P, SLOTS])
        cen, sq = dst_rows, self_rows
        var = sb("var", [P, SLOTS])
        std = sb("std", [P, SLOTS])
        rstd = sb("rstd", [P, SLOTS])
        x1 = sb("x1", [P, SLOTS, LW])
        y_out = sb("y_out", [P, SLOTS, D])
        dst_stage = [sb(f"dst_stage{i}", [P, 2 * GC], U32) for i in range(2)]
        g1 = [gx[i][:, :, 0:LW] for i in range(2)]

        acc = ctx.enter_context(nc.psum_tensor("acc", [P, 2, 512], F32))
        sums = [acc[:, 0, 0:PARTS[0] * LW], acc[:, 0, PARTS[0] * LW:LEFT * LW], acc[:, 1, 0:PARTS[2] * LW]]
        rep_ps = ctx.enter_context(nc.psum_tensor("rep_ps", [P, 2, 512], F32))
        comp_ps = ctx.enter_context(nc.psum_tensor("comp_ps", [P, 512], F32))
        xs_ps = ctx.enter_context(nc.psum_tensor("xs_ps", [P, 512], F32))
        msgT_ps = ctx.enter_context(nc.psum_tensor("msgT_ps", [P, P], F32))
        rel_msg_ps = ctx.enter_context(nc.psum_tensor("rel_msg_ps", [P, 4, GC, D], F32))
        rel_ps, msg_ps = rel_msg_ps[:, 0:2, :, :], rel_msg_ps[:, 2:4, :, :]

        pool_const = sem("pool_const")
        dve_const = sem("dve_const")
        x_padded = sem("x_padded")
        edges_padded = sem("edges_padded")
        idx_loaded = sem("idx_loaded")
        typ_loaded = sem("typ_loaded")
        wgt_loaded = sem("wgt_loaded")
        x_loaded = sem("x_loaded")
        par_loaded = sem("par_loaded")
        small_loaded = sem("small_loaded")
        base_loaded = sem("base_loaded")
        types_stored = sem("types_stored")
        chunk_stored = sem("chunk_stored")
        src_stored = sem("src_stored")
        dst_stored = sem("dst_stored")
        self_stored = sem("self_stored")
        nat_ready = sem("nat_ready")
        typ_ready = sem("typ_ready")
        keys_ready = sem("keys_ready")
        edges_turned = sem("edges_turned")
        x_turned = sem("x_turned")
        xT_copied = sem("xT_copied")
        x_spread = sem("x_spread")
        products_ready = sem("products_ready")
        tab_ready = sem("tab_ready")
        idx_copied = sem("idx_copied")
        w_copied = sem("w_copied")
        neg_k_ready = sem("neg_k_ready")
        dve = sem("dve")
        parts_ready = sem("parts_ready")
        weights_ready = sem("weights_ready")
        types_loaded = [sem(f"types_loaded{i}") for i in range(2)]
        type_hot_ready = sem("type_hot_ready")
        staged = sem("staged")
        turns = sem("turns")
        gathered = [sem(f"gathered{i}") for i in range(2)]
        comp_ready = sem("comp_ready")
        comp_copied = sem("comp_copied")
        xs_ready = sem("xs_ready")
        xs_copied = sem("xs_copied")
        rel_ready = sem("rel_ready")
        rep_ready = sem("rep_ready")
        z_ready = sem("z_ready")
        msgT_ready = sem("msgT_ready")
        msgT_copied = sem("msgT_copied")
        msg_ready = sem("msg_ready")
        yr_ready = sem("yr_ready")
        prod_ready = sem("prod_ready")
        score_ready = sem("score_ready")
        relu_ready = sem("relu_ready")
        att_ready = sem("att_ready")
        value_ready = sem("value_ready")
        term1_ready = sem("term1_ready")
        rest_ready = sem("rest_ready")
        term2_ready = sem("term2_ready")
        terms_ready = sem("terms_ready")
        dist_ready = sem("dist_ready")
        hot_ready = sem("hot_ready")
        slot_ready = sem("slot_ready")
        spread_ready = sem("spread_ready")
        scattered = sem("scattered")
        counted = sem("counted")
        grew_ready = sem("grew_ready")
        grew_at_ready = sem("grew_at_ready")
        last_kept = sem("last_kept")
        last_ready = sem("last_ready")
        tail_hot_ready = sem("tail_hot_ready")
        tail_counted = sem("tail_counted")
        tail_read = sem("tail_read")
        rows_in = [sem(f"rows_in{i}") for i in range(QS)]
        last_src_ready = sem("last_src_ready")
        curr_in = [sem(f"curr_in{i}") for i in range(QS)]
        acc_read = sem("acc_read")
        var_ready = sem("var_ready")
        std_ready = sem("std_ready")
        x1_ready = sem("x1_ready")
        x1_stored = sem("x1_stored")
        staged1 = sem("staged1")
        gathered1 = [sem(f"gathered1{i}") for i in range(2)]
        slot_ready1 = sem("slot_ready1")
        dist_ready1 = sem("dist_ready1")
        wx_ready = sem("wx_ready")
        term1_ready1 = sem("term1_ready1")
        rest_ready1 = sem("rest_ready1")
        term2_ready1 = sem("term2_ready1")
        wx_terms_ready1 = sem("wx_terms_ready1")
        hot_ready1 = sem("hot_ready1")
        spread_ready1 = sem("spread_ready1")
        scattered1 = sem("scattered1")
        out_ready = sem("out_ready")
        out_stored = sem("out_stored")

        block = ctx.enter_context(nc.Block())

        def pairs(eng, first, last, step):
            with eng.Fori(first // 2, last // 2) as i:
                for b in range(2):
                    step(2 * i + b, b)

        def slots(eng, slot, after={}):
            def peeled(ts):
                for t in ts:
                    slot(t, t % 2, t // 2, There(t <= GROUPS - 2, t < GROUPS, 1 <= t <= GROUPS, 2 <= t <= GROUPS + 1,
                                                 3 <= t <= GROUPS + 2, 4 <= t < GROUPS + 4 - TG))
                    if t in after:
                        after[t]()

            peeled(range(6))
            with eng.Fori(3, GROUPS // 2 - 1) as i:
                for b in range(2):
                    slot(2 * i + b, b, i, There(True, True, True, True, True, True))
            peeled(range(GROUPS - 2, GROUPS + 3))

        @block.sync
        def _(sp):
            nblk = "(b r) e -> r b e"

            def load_edges(tile, ap, s):
                full = ap[0:(NBLK - 1) * BR * P].rearrange("(b r e) -> r b e", r=BR, e=P)
                sp.dma_start(tile[:, 0:NBLK - 1, :], full).then_inc(s, 16)
                rest = ap[(NBLK - 1) * BR * P:FULL * P].rearrange("(r e) -> r e", e=P)
                sp.dma_start(tile[0:LASTROWS, NBLK - 1, :], rest).then_inc(s, 16)
                sp.dma_start(tile[LASTROWS:BR, NBLK - 1, 0:TAIL],
                             ap[FULL * P:E].rearrange("(r e) -> r e", r=1)).then_inc(s, 16)

            sp.wait_ge(x_padded, 1)
            sp.dma_start(x_sb[0:ROWS, :, :], x.rearrange("(r s) f -> r s f", s=SLOTS)).then_inc(x_loaded, 16)
            for a, w in enumerate((a1_w, a2_w, self_w)):
                sp.dma_start(w_raw[:, a, :], w).then_inc(par_loaded, 16)
            sp.dma_start(bias_t[:, 0, :], a1_b.rearrange("(r f) -> r f", r=1).to_broadcast([P, D])).then_inc(par_loaded, 16)
            sp.dma_start(bias_t[:, 1, :], a2_b.rearrange("(r f) -> r f", r=1).to_broadcast([P, D])).then_inc(par_loaded, 16)
            sp.wait_ge(edges_padded, 4)
            load_edges(src_n, src, idx_loaded)
            load_edges(dst_n, dst, idx_loaded)
            load_edges(typ_n, etype, typ_loaded)
            load_edges(wgt_n, weight, wgt_loaded)
            sp.dma_start(small_raw[:, 0:D], rel_emb).then_inc(small_loaded, 16)
            sp.dma_start(small_raw[:, D:D + NB], w_comp).then_inc(small_loaded, 16)
            sp.dma_start(base_w[:, :, :], bases.rearrange("b i o -> (b i) o").rearrange("(k m) o -> m k o", k=KT)
                         ).then_inc(base_loaded, 16)
            sp.wait_ge(typ_ready, 1)
            sp.dma_start(type_tab.rearrange(nblk, b=NBLK), typ_nb[:, :, :]).then_inc(types_stored, 16)
            sp.wait_ge(x_spread, BPT)

            def store_slots(tab, tile, ss, stored):
                sp.dma_start(tab.rearrange("(r s) f -> r s f", s=SLOTS)[:, ss, :], tile[:, ss, :]).then_inc(stored, 16)

            for first, last in zip(TAB_CUTS[:-1], TAB_CUTS[1:]):
                ss = slice(4 * first, min(4 * last, SLOTS))
                sp.wait_ge(tab_ready, last)
                store_slots(src_tab, src_rows, ss, src_stored)
                store_slots(dst_tab, dst_rows, ss, dst_stored)
            store_slots(self_tab, self_rows, slice(0, SLOTS), self_stored)
            sp.wait_ge(keys_ready, 1)
            sp.dma_start(chunk_tab.rearrange(nblk, b=NBLK), chunk_n[:, :, :]).then_inc(chunk_stored, 16)

            sp.wait_ge(types_stored, 16)

            def load_types(t, b):
                need(sp, type_hot_ready, t - 1)
                sp.dma_start(types_b[b][:, :],
                             type_tab[bass.ds(t * GC, GC), :].rearrange("(a c) e -> a (c e)", a=1).to_broadcast([R, GC * P])
                             ).then_inc(types_loaded[b], 16)

            load_types(0, 0)
            load_types(1, 1)
            pairs(sp, 2, GROUPS, load_types)

            for q in range(QS):
                ss = slice(q * SQ, (q + 1) * SQ)
                sp.wait_ge(x1_ready, q + 1)
                sp.dma_start(x1_tab.rearrange("(r s) f -> r s f", s=SLOTS)[:, ss, :], x1[:, ss, :]).then_inc(x1_stored, 16)
            for n, ss in enumerate(BANKS):
                sp.wait_ge(out_ready, n + 1)
                sp.dma_start(out.rearrange("(r s) f -> r s f", s=SLOTS)[:, ss, :], y_out[0:ROWS, ss, :]
                             ).then_inc(out_stored, 16)
            for s, n in ((types_stored, 1), (chunk_stored, 1), (src_stored, PIECES), (dst_stored, PIECES), (self_stored, 1),
                         (x1_stored, QS), (out_stored, 2)):
                sp.wait_ge(s, 16 * n)

        @block.gpsimd
        def _(pool):
            g = nc.gpsimd
            small = dict(allow_small_or_imprecise_dtypes=True)
            g.iota(ident_i[:, :], [[1, P]], base=0, channel_multiplier=-1).then_inc(pool_const, 1)
            g.iota(rep_i[:, :, :], [[1, NB], [0, D]], base=0, channel_multiplier=-1).then_inc(pool_const, 1)
            g.iota(iota_k[:, :], [[1, 3 * P]], base=0, channel_multiplier=0, **small).then_inc(pool_const, 1)
            g.iota(iota_lx[:, :, :], [[1, WIDE], [0, LW]], base=0, channel_multiplier=0, **small).then_inc(pool_const, 1)
            g.iota(chunk_no[:, :], [[1, CH]], base=0, channel_multiplier=0, **small).then_inc(pool_const, 1)
            g.iota(type_id[:, :], [[0, 1]], base=0, channel_multiplier=1, **small).then_inc(pool_const, 1)
            g.iota(node_id[:, :], [[1, SLOTS]], base=0, channel_multiplier=SLOTS, **small).then_inc(pool_const, 1)
            g.iota(pos_key[:, :], [[KEY, P]], base=0, channel_multiplier=0, **small).then_inc(pool_const, 1)

            pool.wait_ge(idx_loaded, 2 * 48)
            g.tensor_copy(src_nf[:, :, :], src_n[:, :, :]).then_inc(nat_ready, 1)
            g.tensor_copy(chunk_n[:, :, 0:P], dst_n[:, :, :]).then_inc(nat_ready, 1)
            pool.wait_ge(typ_loaded, 48)
            g.tensor_copy(typ_nb[:, :, :], typ_n[:, :, :]).then_inc(typ_ready, 1)
            pool.wait_ge(nat_ready, 1)
            g.tensor_tensor(chunk_n[:, :, P:2 * P], src_nf[:, :, :],
                            pos_key[0:BR, :].unsqueeze(1).to_broadcast([BR, NBLK, P]), ALU.add).then_inc(keys_ready, 1)

            pool.wait_ge(src_stored, 16 * PIECES)
            pool.wait_ge(dst_stored, 16 * PIECES)
            pool.wait_ge(idx_copied, 1)

            def in_pairs(stage_pair, gather):
                def pair(p, c, ahead=True):
                    gather(p, c, 0)
                    if ahead:
                        stage_pair(p + 1, 1 - c, p)
                    gather(p, c, 1)

                last = GROUPS // 2 - 1
                stage_pair(0, 0, 0)
                pair(0, 0)
                with pool.Fori(0, (last - 1) // 2) as i:
                    for u in range(2):
                        pair(2 * i + (u + 1), (u + 1) % 2)
                pair(last, last % 2, ahead=False)

            def stage_pair0(p, c, done):
                for b in range(2):
                    need(pool, gathered[b], done * (32 * GC))
                g.tensor_copy(stage[c][:, :, :], idx_all[:, :, bass.ds(p * 2 * GC, 2 * GC)]).then_inc(staged, 1)

            def gather0(p, c, b):
                t = 2 * p + b
                need(pool, prod_ready, t - 1)
                need(pool, xs_ready, t - 1)
                pool.wait_ge(staged, p + 1)
                pool.sem_inc(turns, 1)
                for j in range(GC):
                    at = slice(b * GC + j, b * GC + j + 1)
                    g.indirect_dma_start(gx[b][:, j, :], None, src_tab, bass.IndirectOffsetOnAxis(stage[c][:, 0, at], 0)
                                         ).then_inc(gathered[b], 16)
                    g.indirect_dma_start(gy[b][:, j, :], None, dst_tab, bass.IndirectOffsetOnAxis(stage[c][:, 1, at], 0)
                                         ).then_inc(gathered[b], 16)

            in_pairs(stage_pair0, gather0)

            pool.wait_ge(chunk_stored, 16)
            pool.wait_ge(self_stored, 16)
            pool.wait_ge(last_ready, 1)
            for s in range(SLOTS):
                g.indirect_dma_start(rows[:, s, :], None, chunk_tab,
                                     bass.IndirectOffsetOnAxis(last_chunk[:, s:s + 1], 0)).then_inc(rows_in[s // SQ], 16)
            for s in range(SLOTS):
                if s % SQ == 0:
                    pool.wait_ge(last_src_ready, s // SQ + 1)
                g.indirect_dma_start(curr[:, s, :], None, self_tab,
                                     bass.IndirectOffsetOnAxis(last_src[:, s:s + 1], 0)).then_inc(curr_in[s // SQ], 16)

            pool.wait_ge(x1_stored, 16 * QS)

            def stage_pair1(p, c, done):
                for b in range(2):
                    need(pool, gathered1[b], done * (16 * GC))
                g.tensor_copy(dst_stage[c][:, :], idx_all[:, 1, bass.ds(p * 2 * GC, 2 * GC)]).then_inc(staged1, 1)

            def gather1(p, c, b):
                t = 2 * p + b
                need(pool, wx_ready, t - 1)
                pool.wait_ge(staged1, p + 1)
                pool.sem_inc(turns, 1)
                for j in range(GC):
                    at = slice(b * GC + j, b * GC + j + 1)
                    g.indirect_dma_start(g1[b][:, j, :], None, x1_tab, bass.IndirectOffsetOnAxis(dst_stage[c][:, at], 0)
                                         ).then_inc(gathered1[b], 16)

            in_pairs(stage_pair1, gather1)

        @block.tensor
        def _(pe):
            te = nc.tensor

            def clear_sums():
                for h in range(2):
                    te.matmul(acc[:, h, :], zeros[:, :], zrow[:, :], start=True, stop=True)

            pe.wait_ge(dve_const, 1)
            pe.wait_ge(x_loaded, 16)
            turned = [xs_ps[:, :], rel_msg_ps[:, :, :, :].rearrange("p a c f -> p (a c f)")]
            for j in range(NT):
                ns = min(4, SLOTS - 4 * j)
                te.transpose(turned[j // 4][0:ns * D, (j % 4) * P:(j % 4 + 1) * P],
                             x_sb[:, 4 * j:4 * j + ns, :].rearrange("p s f -> p (s f)"), ident[:, :]
                             ).then_inc(x_turned, 1)
            pe.wait_ge(weights_ready, 1)
            for j in range(NT):
                ns = min(4, SLOTS - 4 * j)
                pe.wait_ge(xT_copied, 1 if j < 4 else 3)
                if j >= 2:
                    pe.wait_ge(tab_ready, j - 1)
                te.matmul(rep_ps[:, j % 2, 0:ns * TABW], xT[0:ns * D, j, :],
                          prod_w[0:ns * D, 0:ns, :].rearrange("p s c -> p (s c)"),
                          start=True, stop=True).then_inc(products_ready, 1)
            pe.wait_ge(nat_ready, 2)
            pe.wait_ge(wgt_loaded, 48)
            for ps, tile in ((acc[:, 0, :], src_nf[:, :, :]), (acc[:, 1, :], chunk_n[:, :, 0:P]),
                             (comp_ps[:, :], wgt_n[:, :, :])):
                for b in range(NBLK):
                    m = te.transpose(ps[:, b * BR:(b + 1) * BR], tile[:, b, :], ident[0:BR, 0:BR])
                m.then_inc(edges_turned, 1)
            pe.wait_ge(idx_copied, 1)
            pe.wait_ge(tab_ready, NT)
            pe.wait_ge(w_copied, 1)
            pe.wait_ge(parts_ready, 1)
            pe.wait_ge(base_loaded, 16)

            def look_up_comp(t, b):
                pe.wait_ge(type_hot_ready, t + 1)
                need(pe, comp_copied, t)
                te.matmul(comp_ps[0:3 * NB, :], comp_p[:, :, :].rearrange("r a c -> r (a c)"), type_hot[b][:, :],
                          start=True, stop=True).then_inc(comp_ready, 1)

            def turn_x(t, b, chunks, got):
                if chunks[0] == 0:
                    need(pe, xs_copied, t)
                    pe.wait_ge(gathered[b], got)
                for j in chunks:
                    m = te.transpose(xs_ps[:, j * P:(j + 1) * P], gx[b][:, j, 0:P], ident[:, :])
                if chunks[-1] == GC - 1:
                    m.then_inc(xs_ready, 1)

            def look_up_rel(t, b):
                need(pe, yr_ready, t)
                need(pe, value_ready, t - 2)
                for j in range(GC):
                    for a in range(3):
                        m = te.matmul(rel_ps[:, b, j, :], type_hot[b][:, j * P:(j + 1) * P], rel_p[:, a, :],
                                      start=(a == 0), stop=(a == 2))
                m.then_inc(rel_ready, 1)

            def repeat_comp(t, b, k):
                if k == 0:
                    pe.wait_ge(comp_copied, t + 1)
                need(pe, z_ready, t * KT + k - 1)
                te.matmul(rep_ps[:, k % 2, :], rep[:, k * P:(k + 1) * P], compT[b][:, :],
                          start=True, stop=True).then_inc(rep_ready, 1)

            def add_part(b, j, h):
                cols = PARTS[h] * LW
                for a in range(TERMS):
                    m = te.matmul(sums[h], row_hot[b][:, j, h * P:(h + 1) * P], spread[b][:, j, a, 0:cols],
                                  start=False, stop=True, skip_group_check=True)
                return m

            def scatter(t, b, j, hs):
                if hs[0] == 0:
                    if j % 2 == 0:
                        pe.wait_ge(hot_ready, 2 * t + (j // 2 + 1))
                    pe.wait_ge(spread_ready, t * GC + j + 1)
                    need(pe, counted, t * GC + j)
                for h in hs:
                    m = add_part(b, j, h)
                if hs[-1] == 2:
                    m.then_inc(scattered, 1)

            def messages(t, b, k):
                if k == 0:
                    pe.wait_ge(z_ready, (t + 1) * KT)
                    need(pe, msgT_copied, t)
                for j in range(GC):
                    m = te.matmul(msgT_ps[j * D:(j + 1) * D, :], base_w[:, k, :], z[b][:, k, j * P:(j + 1) * P],
                                  start=(k == 0), stop=(k == KT - 1))
                if k == KT - 1:
                    m.then_inc(msgT_ready, 1)

            def turn_messages(t, b):
                pe.wait_ge(msgT_copied, t + 1)
                te.transpose(msg_ps[:, b, :, :].rearrange("p c f -> p (c f)"), msgT[b][:, :], ident[:, :]
                             ).then_inc(msg_ready, 1)

            def slot(t, b, half, has):
                got = (half + 1 if b == 0 else half + 2) * (32 * GC)
                for j in range(GC):
                    if has.new:
                        repeat_comp(t, b, j)
                    if has.turn:
                        messages(t - 1, 1 - b, j)
                    if has.ahead and j == 1:
                        look_up_comp(t + 1, 1 - b)
                    if has.ahead and j >= 2:
                        turn_x(t + 1, 1 - b, (0, 1) if j == 2 else (2, 3), got)
                    if has.ahead and j == GC - 1:
                        look_up_rel(t + 1, 1 - b)
                    if has.spread:
                        scatter(t - 3, 1 - b, j, (0, 1))
                    if has.turn and j == GC - 1:
                        turn_messages(t - 1, 1 - b)
                    if has.spread:
                        scatter(t - 3, 1 - b, j, (2,))

            look_up_comp(0, 0)
            turn_x(0, 0, range(GC), 32 * GC)
            look_up_rel(0, 0)

            def count_tail():
                pe.wait_ge(tail_hot_ready, TB + 1)
                for c in range(TC):
                    hot = tail_hot[c // (TC // TB)][:, c % (TC // TB), :]
                    for h, n in enumerate(PARTS):
                        at = c * SLOTS + sum(PARTS[:h])
                        m = te.matmul(acc[:, 0, at:at + n], hot[:, h * P:(h + 1) * P], tail_slot_hot[:, c, 0:n],
                                      start=True, stop=True)
                m.then_inc(tail_counted, 1)

            def start_sums():
                pe.wait_ge(tail_read, 1)
                clear_sums()

            slots(pe, slot, {1: count_tail, 2: start_sums})

            pe.wait_ge(acc_read, 1)
            pe.wait_ge(counted, CH)
            clear_sums()

            def scatter1(t, b):
                pe.wait_ge(hot_ready1, t + 1)
                for j in range(GC):
                    pe.wait_ge(spread_ready1, t * GC + (j + 1))
                    for h in range(3):
                        m = add_part(b, j, h)
                    m.then_inc(scattered1, 1)

            pairs(pe, 0, GROUPS, scatter1)

        @block.scalar
        def _(act):
            sc = nc.scalar

            def copy_comp(t, b):
                act.wait_ge(comp_ready, t + 1)
                need(act, rep_ready, (t - 1) * KT)
                sc.activation(compT[b][:, :], comp_ps[0:3 * NB, :], ACT.Copy).then_inc(comp_copied, 1)

            def copy_xs(t, b):
                act.wait_ge(xs_ready, t + 1)
                need(act, z_ready, (t - 1) * KT)
                sc.activation(xsT[b][:, :], xs_ps[:, :], ACT.Copy).then_inc(xs_copied, 1)

            def count(t, j):
                c = t * GC + j
                act.wait_ge(scattered, c + 1)
                for h, ss in enumerate(BANKS):
                    n = ss.stop - ss.start
                    m = sc.activation(counts[:, bass.ds(c * SLOTS + (SLOTS + ss.start), n)].unsqueeze(2),
                                      acc[:, h, 0:n * LW].rearrange("p (l f) -> p l f", f=LW)[:, :, D:D + 1], ACT.Copy)
                m.then_inc(counted, 1)

            def attention(t, b):
                act.wait_ge(score_ready, t + 1)
                sc.activation(score_r[b][:, :], score[b][:, :], ACT.Relu, scale=float(D) ** -0.5).then_inc(relu_ready, 1)
                act.wait_ge(relu_ready, t + 1)
                need(act, value_ready, t - 1)
                sc.activation(att[b][:, :], score_r[b][:, :], ACT.Tanh).then_inc(att_ready, 1)

            def row_dists(t, b, chunks):
                if chunks[0] == 0:
                    need(act, scattered, (t - 1) * GC)
                for j in chunks:
                    m = sc.activation(row_hot[b][:, j, :], iota_k[:, :], ACT.Abs, bias=neg_k[:, 1, bass.ds(t * GC + j, 1)])
                m.then_inc(dist_ready, 1)

            def row_hots(t, b, n):
                act.wait_ge(dist_ready, 2 * t + (n + 1))
                js = slice(2 * n, 2 * n + 2)
                sc.activation(row_hot[b][:, js, :], row_hot[b][:, js, :], ACT.Relu, bias=ones[:, 0:1], scale=-1.0
                              ).then_inc(hot_ready, 1)

            def slot(t, b, half, has):
                if has.spread:
                    count(t - 3, 0)
                if has.weigh:
                    act.wait_ge(value_ready, t - 1)
                    need(act, spread_ready, (t - 3) * GC)
                    sc.activation(wx_terms[b][:, :, 0, 0:D], wx[b][:, :, 0:D], ACT.Copy).then_inc(term1_ready, 1)
                    row_dists(t - 2, b, (0, 1))
                if has.spread:
                    count(t - 3, 1)
                if has.new:
                    attention(t, b)
                if has.ahead:
                    copy_comp(t + 1, 1 - b)
                if has.weigh:
                    act.wait_ge(rest_ready, t - 1)
                    sc.activation(wx_terms[b][:, :, 1, 0:D], wx_rest[b][:, :, 0:D], ACT.Copy).then_inc(term2_ready, 1)
                    row_dists(t - 2, b, (2, 3))
                if has.spread:
                    count(t - 3, 2)
                if has.weigh:
                    row_hots(t - 2, b, 0)
                if has.turn:
                    act.wait_ge(msgT_ready, t)
                    need(act, msg_ready, t - 2)
                    sc.activation(msgT[1 - b][:, :], msgT_ps[:, :], ACT.Copy).then_inc(msgT_copied, 1)
                if has.ahead:
                    copy_xs(t + 1, 1 - b)
                if has.weigh:
                    row_hots(t - 2, b, 1)
                if has.spread:
                    count(t - 3, 3)

            act.wait_ge(x_turned, 4)
            sc.activation(xT[:, 0:4, :], xs_ps[:, :].rearrange("p (j e) -> p j e", j=4), ACT.Copy).then_inc(xT_copied, 1)
            act.wait_ge(x_turned, NT)
            rest = rel_msg_ps[:, :, :, :].rearrange("p a c f -> p (a c f)").rearrange("p (j e) -> p j e", j=4)
            sc.activation(xT[:, 4:NT - 1, :], rest[:, 0:NT - 5, :], ACT.Copy).then_inc(xT_copied, 1)
            sc.activation(xT[0:D, NT - 1, :], rest[0:D, NT - 5, :], ACT.Copy).then_inc(xT_copied, 1)
            for r in range(BPT):
                sc.activation(src_rows[:, :, r * D:(r + 1) * D], x_sb[:, :, :], ACT.Copy).then_inc(x_spread, 1)

            copy_comp(0, 0)
            act.wait_ge(neg_k_ready, 1)
            copy_xs(0, 0)
            slots(act, slot)

            def norm_root(n, ss):
                act.wait_ge(var_ready, n)
                sc.activation(std[:, ss], var[:, ss], ACT.Sqrt, bias=eps_t[:, 0:1], scale=1.0 / D).then_inc(std_ready, 1)

            for q in range(QS):
                norm_root(q + 1, slice(q * SQ, (q + 1) * SQ))

            def slot1(t, b):
                act.wait_ge(wx_ready, t + 1)
                need(act, spread_ready1, (t - 1) * GC)
                sc.activation(wx_terms[b][:, :, 0, :], wx[b][:, :, :], ACT.Copy).then_inc(term1_ready1, 1)
                need(act, scattered1, (t - 1) * GC)
                for j in range(GC):
                    if j == GC - 1:
                        act.wait_ge(rest_ready1, t + 1)
                        sc.activation(wx_terms[b][:, :, 1, :], wx_rest[b][:, :, :], ACT.Copy).then_inc(term2_ready1, 1)
                    m = sc.activation(row_hot[b][:, j, :], iota_k[:, :], ACT.Abs, bias=neg_k[:, 0, bass.ds(t * GC + j, 1)])
                m.then_inc(dist_ready1, 1)
                act.wait_ge(dist_ready1, t + 1)
                sc.activation(row_hot[b][:, :, :], row_hot[b][:, :, :], ACT.Relu, bias=ones[:, 0:1], scale=-1.0
                              ).then_inc(hot_ready1, 1)

            for t in range(2):
                slot1(t, t)
            pairs(act, 2, GROUPS, slot1)
            norm_root(QS + 1, BANKS[0])
            norm_root(QS + 2, BANKS[1])

        @block.vector
        def _(ve):
            v = nc.vector
            done = [0]

            def link(ins):
                done[0] += 1
                ins.then_inc(dve, 1)
                ve.wait_ge(dve, done[0])

            def slots_b(ap, n=D):
                return ap.unsqueeze(2).to_broadcast([P, ap.shape[1], n])

            v.memset(x_sb[96:P, :, :], 0.0).then_inc(x_padded, 1)
            v.memset(src_n[:, NBLK - 1, :], PAD).then_inc(edges_padded, 1)
            v.memset(dst_n[:, NBLK - 1, :], PAD).then_inc(edges_padded, 1)
            v.memset(typ_n[:, NBLK - 1, :], 0).then_inc(edges_padded, 1)
            v.memset(wgt_n[:, NBLK - 1, :], 0.0).then_inc(edges_padded, 1)
            ve.wait_ge(pool_const, 1)
            v.tensor_scalar(ident[:, :], ident_i[:, :], 0.0, None, ALU.is_equal).then_inc(dve_const, 1)
            v.memset(zeros[:, :], 0.0)
            v.memset(zrow[:, :], 0.0)
            v.memset(eps_t[:, :], EPS)
            v.memset(ones[:, :], 1.0)
            for i in range(2):
                v.memset(wx_terms[i][:, :, 0, D:D + 1], 1.0)
                v.memset(wx_terms[i][:, :, 0, D + 1:LW], 0.0)
                v.memset(wx_terms[i][:, :, 1:TERMS, D:LW], 0.0)
            v.memset(x1[:, :, D:D + 1], 1.0)
            v.memset(x1[:, :, D + 1:LW], 0.0)
            link(v.memset(prod_w[:, :, :], 0.0))
            ve.wait_ge(par_loaded, 5 * 16)
            v.transpose(prod_w[0:D, 0, 0:D], w_raw[:, 0, :])
            v.transpose(prod_w[0:D, 0, D:2 * D], w_raw[:, 1, :])
            link(v.tensor_copy(prod_w[0:D, 0, 2 * D:3 * D], w_raw[:, 2, :]))
            for q in range(1, 4):
                m = v.tensor_copy(prod_w[q * D:(q + 1) * D, q, :], prod_w[0:D, 0, :])
            m.then_inc(weights_ready, 1)
            ve.wait_ge(pool_const, 8)
            link(v.tensor_scalar(rep_i[:, :, :], rep_i[:, :, :], NB - 1, None, ALU.bitwise_and))
            v.tensor_scalar(rep[:, :], rep_i[:, :, :].rearrange("p b f -> p (b f)"), 0.0, None, ALU.is_equal)
            for j in range(NT):
                ns = min(4, SLOTS - 4 * j)
                s = slice(4 * j, 4 * j + ns)
                ve.wait_ge(products_ready, j + 1)
                got = rep_ps[:, j % 2, 0:ns * TABW].rearrange("p (s c) -> p s c", c=TABW)
                bias = [bias_t[:, a, :].unsqueeze(1).to_broadcast([P, ns, D]) for a in range(2)]
                v.tensor_tensor(src_rows[:, s, P:SRCW], got[:, :, 0:D], bias[0], ALU.add)
                v.tensor_tensor(dst_rows[:, s, :], got[:, :, D:2 * D], bias[1], ALU.add)
                v.tensor_copy(self_rows[:, s, :], got[:, :, 2 * D:3 * D]).then_inc(tab_ready, 1)
            for a in range(2):
                ve.wait_ge(edges_turned, a + 1)
                m = v.tensor_copy(idx_all[:, a, :], acc[:, a, 0:CH])
            m.then_inc(idx_copied, 1)
            ve.wait_ge(small_loaded, 32)
            link(v.tensor_copy(small_bf[:, 0, :], small_raw[:, :]))
            link(v.tensor_tensor(small_res[:, 0, :], small_raw[:, :], small_bf[:, 0, :], ALU.subtract))
            link(v.tensor_copy(small_bf[:, 1, :], small_res[:, 0, :]))
            link(v.tensor_tensor(small_res[:, 1, :], small_res[:, 0, :], small_bf[:, 1, :], ALU.subtract))
            link(v.tensor_copy(small_bf[:, 2, :], small_res[:, 1, :]))
            v.tensor_copy(rel_p[:, :, :], small_bf[:, :, 0:D])
            v.tensor_copy(comp_p[:, :, :], small_bf[:, :, D:D + NB]).then_inc(parts_ready, 1)
            ve.wait_ge(edges_turned, 3)
            v.tensor_copy(w_all[:, :], comp_ps[:, 0:CH]).then_inc(w_copied, 1)

            def type_one_hot(t, b, got):
                ve.wait_ge(types_loaded[b], got)
                need(ve, rel_ready, t - 1)
                v.tensor_scalar(type_hot[b][:, :], types_b[b][:, :], type_id[0:R, 0:1], None,
                                ALU.is_equal).then_inc(type_hot_ready, 1)

            type_one_hot(0, 0, 16)
            link(v.tensor_copy(n_f[:, :, :], idx_all[:, :, :]))
            link(v.tensor_scalar(q_i[:, :, :], n_f[:, :, :], float(RECIP), None, ALU.mult))
            link(v.tensor_scalar(q_i[:, :, :], q_i[:, :, :], SHIFT, None, ALU.logical_shift_right))
            link(v.tensor_copy(row_f[:, :, :], q_i[:, :, :]))
            link(v.scalar_tensor_tensor(slot_f[:, :, :], row_f[:, :, :], -float(SLOTS), n_f[:, :, :], ALU.mult, ALU.add))
            link(v.tensor_scalar(n_f[:, :, :], slot_f[:, :, :], float(PARTS[0]), None, ALU.is_ge))
            link(v.scalar_tensor_tensor(part_f[:, :, :], slot_f[:, :, :], float(LEFT), n_f[:, :, :], ALU.is_ge, ALU.add))
            v.scalar_tensor_tensor(k_all[:, :, :], part_f[:, :, :], float(P), row_f[:, :, :], ALU.mult, ALU.add)
            link(v.scalar_tensor_tensor(slot_f[:, :, :], part_f[:, :, :], -float(PARTS[1]), slot_f[:, :, :],
                                        ALU.mult, ALU.add))
            link(v.scalar_tensor_tensor(lo_all[:, :, :], n_f[:, :, :], -float(PARTS[0] - PARTS[1]), slot_f[:, :, :],
                                        ALU.mult, ALU.add))
            v.tensor_scalar(neg_k[:, :, :], k_all[:, :, :], -1.0, None, ALU.mult).then_inc(neg_k_ready, 1)

            def times_x(t, b, k):
                ve.wait_ge(rep_ready, t * KT + (k + 1))
                if k == 0:
                    ve.wait_ge(xs_copied, t + 1)
                    need(ve, msgT_ready, t - 1)
                v.tensor_tensor(z[b][:, k, :], rep_ps[:, k % 2, :], xsT[b][:, :], ALU.mult).then_inc(z_ready, 1)

            def weigh(t, b):
                ve.wait_ge(msg_ready, t + 1)
                ve.wait_ge(att_ready, t + 1)
                need(ve, term1_ready, t - 1)
                v.tensor_tensor(wx[b][:, :, 0:D], msg_ps[:, b, :, :],
                                att[b][:, :].unsqueeze(2).to_broadcast([P, GC, D]), ALU.mult).then_inc(value_ready, 1)

            def take_rest(t, b):
                ve.wait_ge(term1_ready, t + 1)
                need(ve, term2_ready, t - 1)
                v.tensor_tensor(wx_rest[b][:, :, 0:D], wx[b][:, :, 0:D], wx_terms[b][:, :, 0, 0:D], ALU.subtract
                                ).then_inc(rest_ready, 1)

            def take_last_term(t, b):
                ve.wait_ge(term2_ready, t + 1)
                v.tensor_tensor(wx_terms[b][:, :, 2, 0:D], wx_rest[b][:, :, 0:D], wx_terms[b][:, :, 1, 0:D], ALU.subtract
                                ).then_inc(terms_ready, 1)

            def slot_one_hots(t, b, a, chunks, ready):
                for j in chunks:
                    m = v.tensor_scalar(slot_hot[b][:, j, :], iota_lx[:, :, :].rearrange("p l f -> p (l f)"),
                                        lo_all[:, a, bass.ds(t * GC + j, 1)], None, ALU.is_equal)
                m.then_inc(ready, 1)

            def spread_chunk(b, j, ready):
                v.tensor_tensor(spread[b][:, j, :, :].rearrange("p a (l f) -> p a l f", f=LW),
                                slot_hot[b][:, j, :].rearrange("p (l f) -> p l f", f=LW).unsqueeze(1)
                                .to_broadcast([P, TERMS, WIDE, LW]),
                                wx_terms[b][:, j, :, :].unsqueeze(2).to_broadcast([P, TERMS, WIDE, LW]),
                                ALU.mult).then_inc(ready, 1)

            def spread_msg(t, b, j):
                if j == 0:
                    ve.wait_ge(terms_ready, t + 1)
                    ve.wait_ge(slot_ready, 2 * t + 2)
                    need(ve, scattered, (t - 1) * GC)
                spread_chunk(b, j, spread_ready)

            def find_growth(t, b):
                ve.wait_ge(counted, (t + 1) * GC)
                after = counts[:, bass.ds(t * GC * SLOTS + SLOTS, GC * SLOTS)].rearrange("p (c s) -> p c s", s=SLOTS)
                prior = counts[:, bass.ds(t * GC * SLOTS, GC * SLOTS)].rearrange("p (c s) -> p c s", s=SLOTS)
                v.tensor_tensor(grew[b][:, :, :], after, prior, ALU.is_gt).then_inc(grew_ready, 1)

            def number_growth(t, b):
                ve.wait_ge(grew_ready, t + 1)
                v.tensor_tensor(grew_at[b][:, :, :], grew[b][:, :, :],
                                chunk_no[:, bass.ds(t * GC, GC)].unsqueeze(2).to_broadcast([P, GC, SLOTS]), ALU.mult
                                ).then_inc(grew_at_ready, 1)

            def keep_last(t, b):
                ve.wait_ge(grew_at_ready, t + 1)
                need(ve, last_kept, t)
                v.tensor_tensor(last_of[:, :, :], last_of[:, :, :], grew_at[b][:, :, :], ALU.max).then_inc(last_kept, 1)

            def slot(t, b, half, has):
                if has.spread:
                    spread_msg(t - 3, 1 - b, 0)
                if has.weigh:
                    weigh(t - 2, b)
                if has.new:
                    times_x(t, b, 0)
                    ve.wait_ge(rel_ready, t + 1)
                    ve.wait_ge(gathered[b], (half + 1) * (32 * GC))
                    v.tensor_tensor(yr[b][:, :, :], rel_ps[:, b, :, :], gy[b][:, :, :], ALU.add).then_inc(yr_ready, 1)
                if has.count:
                    find_growth(t - 4, b)
                if has.ahead:
                    type_one_hot(t + 1, 1 - b, (half + 1 if b == 1 else half) * 16 + 16)
                if has.spread:
                    spread_msg(t - 3, 1 - b, 1)
                if has.new:
                    ve.wait_ge(yr_ready, t + 1)
                    v.tensor_tensor(prod[b][:, :, :], yr[b][:, :, :], gx[b][:, :, P:SRCW], ALU.mult
                                    ).then_inc(prod_ready, 1)
                    times_x(t, b, 1)
                    ve.wait_ge(prod_ready, t + 1)
                    need(ve, relu_ready, t - 1)
                    v.tensor_reduce(score[b][:, :], prod[b][:, :, :], AX, ALU.add).then_inc(score_ready, 1)
                if has.weigh:
                    take_rest(t - 2, b)
                if has.count:
                    number_growth(t - 4, b)
                if has.weigh:
                    slot_one_hots(t - 2, b, 1, (0, 1), slot_ready)
                if has.spread:
                    spread_msg(t - 3, 1 - b, 2)
                if has.new:
                    times_x(t, b, 2)
                if has.count:
                    keep_last(t - 4, b)
                if has.weigh:
                    slot_one_hots(t - 2, b, 1, (2, 3), slot_ready)
                if has.spread:
                    spread_msg(t - 3, 1 - b, 3)
                if has.weigh:
                    take_last_term(t - 2, b)
                if has.new:
                    times_x(t, b, 3)

            ve.wait_ge(src_stored, 16 * PIECES)
            v.memset(counts[:, 0:SLOTS], 0.0)
            v.memset(last_of[:, :, :], 0.0)

            def tail_one_hots(qs):
                n = TC // TB
                for q in qs:
                    v.tensor_tensor(tail_hot[q], iota_k[:, :].unsqueeze(1).to_broadcast([P, n, 3 * P]),
                                    k_all[:, 1, CH - TC + q * n:CH - TC + (q + 1) * n].unsqueeze(2)
                                    .to_broadcast([P, n, 3 * P]), ALU.is_equal).then_inc(tail_hot_ready, 1)

            def find_tail_last():
                ve.wait_ge(tail_counted, 1)
                link(v.tensor_scalar(tail_grew, acc[:, 0, 0:TC * SLOTS].rearrange("p (c s) -> p c s", s=SLOTS), 0.0, None,
                                     ALU.is_gt))
                link(v.tensor_tensor(tail_at, tail_grew, chunk_no[:, CH - TC:CH].unsqueeze(2).to_broadcast([P, TC, SLOTS]),
                                     ALU.mult))
                v.tensor_reduce(tail_last[:, :], tail_at.rearrange("p c s -> p s c"), AX, ALU.max).then_inc(tail_read, 1)

            def find_last_chunk():
                ve.wait_ge(last_kept, GROUPS - TG)
                link(v.tensor_reduce(last_f[:, :], last_of[:, :, :].rearrange("p c s -> p s c"), AX, ALU.max))
                link(v.tensor_tensor(last_f[:, :], last_f[:, :], tail_last[:, :], ALU.max))
                v.tensor_copy(last_chunk[:, :], last_f[:, :]).then_inc(last_ready, 1)

            def find_last_src(q):
                ss = slice(q * SQ, (q + 1) * SQ)
                ve.wait_ge(rows_in[q], 16 * SQ)
                for s in range(q * SQ, (q + 1) * SQ):
                    m = v.scalar_tensor_tensor(keyed[:, s, :], rows[:, s, 0:P], node_id[:, s:s + 1], rows[:, s, P:2 * P],
                                               ALU.is_equal, ALU.mult)
                link(m)
                link(v.tensor_reduce(key_f[:, ss], keyed[:, ss, :], AX, ALU.max))
                link(v.tensor_copy(key_u[:, ss], key_f[:, ss]))
                v.tensor_scalar(last_src[:, ss], key_u[:, ss], KEY - 1, None, ALU.bitwise_and).then_inc(last_src_ready, 1)

            v.tensor_tensor(tail_slot_hot, iota_k[:, 0:WIDE].unsqueeze(1).to_broadcast([P, TC, WIDE]),
                            lo_all[:, 1, CH - TC:CH].unsqueeze(2).to_broadcast([P, TC, WIDE]), ALU.is_equal
                            ).then_inc(tail_hot_ready, 1)
            tail_one_hots((0, 1))

            def two_pieces():
                find_last_src(2)
                find_last_src(3)

            slots(ve, slot, {0: lambda: tail_one_hots((2, 3)), 1: find_tail_last, GROUPS - 2: find_last_chunk,
                             GROUPS - 1: lambda: find_last_src(0), GROUPS: lambda: find_last_src(1),
                             GROUPS + 1: two_pieces, GROUPS + 2: lambda: find_last_src(4)})

            ve.wait_ge(scattered, CH)
            ve.wait_ge(counted, CH)
            v.tensor_scalar(has_in[:, :], counts[:, CH * SLOTS:(CH + 1) * SLOTS], 0.0, None, ALU.is_gt)
            for h, ss in enumerate(BANKS):
                m = v.tensor_copy(h0[:, ss, :], acc[:, h, 0:(ss.stop - ss.start) * LW]
                                  .rearrange("p (l f) -> p l f", f=LW)[:, :, 0:D])
            link(m)
            v.memset(score[0][:, :], 0.0).then_inc(acc_read, 1)

            def layer_norm(h, o, ss, n):
                link(v.tensor_reduce(mean[:, ss], h[:, ss, :], AX, ALU.add))
                link(v.tensor_scalar(mean[:, ss], mean[:, ss], 1.0 / D, None, ALU.mult))
                link(v.tensor_tensor(cen[:, ss, :], h[:, ss, :], slots_b(mean[:, ss]), ALU.subtract))
                link(v.tensor_tensor(sq[:, ss, :], cen[:, ss, :], cen[:, ss, :], ALU.mult))
                v.tensor_reduce(var[:, ss], sq[:, ss, :], AX, ALU.add).then_inc(var_ready, 1)
                ve.wait_ge(std_ready, n)
                link(v.reciprocal(rstd[:, ss], std[:, ss]))
                link(v.tensor_tensor(o[:, ss, 0:D], cen[:, ss, :], slots_b(rstd[:, ss]), ALU.mult))

            for q in range(QS):
                ss = slice(q * SQ, (q + 1) * SQ)
                ve.wait_ge(curr_in[q], 16 * SQ)
                link(v.tensor_tensor(h1[:, ss, :], h0[:, ss, :], curr[:, ss, :], ALU.add))
                link(v.scalar_tensor_tensor(h0[:, ss, :], h1[:, ss, :], 0.0, slots_b(has_in[:, ss]), ALU.max, ALU.mult))
                link(v.tensor_tensor(h1[:, ss, :], h0[:, ss, :], x_sb[:, ss, :], ALU.add))
                layer_norm(h1, x1, ss, q + 1)
                v.memset(score[0][:, :], 0.0).then_inc(x1_ready, 1)

            def spread_wx(t, b, j):
                if j == 0:
                    ve.wait_ge(wx_terms_ready1, t + 1)
                    ve.wait_ge(slot_ready1, 2 * t + 2)
                    need(ve, scattered1, (t - 1) * GC)
                spread_chunk(b, j, spread_ready1)

            def slot1(t, b, half, new=True, old=True):
                if new:
                    ve.wait_ge(gathered1[b], (half + 1) * (16 * GC))
                    v.tensor_tensor(wx[b][:, :, :], g1[b][:, :, :],
                                    w_all[:, bass.ds(t * GC, GC)].unsqueeze(2).to_broadcast([P, GC, LW]), ALU.mult
                                    ).then_inc(wx_ready, 1)
                if old:
                    spread_wx(t - 1, 1 - b, 0)
                if new:
                    slot_one_hots(t, b, 0, (0, 1), slot_ready1)
                if old:
                    spread_wx(t - 1, 1 - b, 1)
                if new:
                    ve.wait_ge(term1_ready1, t + 1)
                    v.tensor_tensor(wx_rest[b][:, :, :], wx[b][:, :, :], wx_terms[b][:, :, 0, :], ALU.subtract
                                    ).then_inc(rest_ready1, 1)
                if old:
                    spread_wx(t - 1, 1 - b, 2)
                if new:
                    slot_one_hots(t, b, 0, (2, 3), slot_ready1)
                if old:
                    spread_wx(t - 1, 1 - b, 3)
                if new:
                    ve.wait_ge(term2_ready1, t + 1)
                    v.tensor_tensor(wx_terms[b][:, :, 2, :], wx_rest[b][:, :, :], wx_terms[b][:, :, 1, :], ALU.subtract
                                    ).then_inc(wx_terms_ready1, 1)

            slot1(0, 0, 0, old=False)
            for t in range(1, 4):
                slot1(t, t % 2, t // 2)
            with ve.Fori(1, GROUPS // 4) as i:
                for u in range(4):
                    slot1(4 * i + u, u % 2, 2 * i + u // 2)
            slot1(GROUPS, 0, GROUPS // 2, new=False)

            ve.wait_ge(scattered1, CH)
            for h, ss in enumerate(BANKS):
                n = ss.stop - ss.start
                part = acc[:, h, 0:n * LW].rearrange("p (l f) -> p l f", f=LW)
                v.tensor_tensor(h0[:, ss, :], part[:, :, 0:D], x1[:, ss, 0:D], ALU.add)
                m = v.tensor_tensor(h1[:, ss, :], x1[:, ss, 0:D], part[:, :, D:D + 1].to_broadcast([P, n, D]), ALU.mult)
            link(m)
            link(v.tensor_tensor(h0[:, :, :], h0[:, :, :], h1[:, :, :], ALU.subtract))
            for n, ss in enumerate(BANKS):
                layer_norm(h0, y_out, ss, QS + n + 1)
                v.memset(score[0][:, :], 0.0).then_inc(out_ready, 1)


_INS = ["x", "src", "dst", "edge_type_86", "edge_weight", "L0_gnn_weight", "L0_gnn_w_comp", "L0_gnn_self_loop_weight",
        "L0_gnn_A1_w", "L0_gnn_A1_b", "L0_gnn_A2_w", "L0_gnn_A2_b", "L0_gnn_rel_emb"]


def kernel(**inputs):
    import numpy as _np
    import concourse.bacc as _bacc
    from concourse import mybir as _mybir
    from concourse.bass_utils import run_bass_kernel_spmd as _run

    nc = _bacc.Bacc("TRN2", target_bir_lowering=False, num_devices=1)
    arrays, args = {}, []
    for name in _INS:
        a = _np.ascontiguousarray(inputs[name])
        arrays[f"in_{name}_dram"] = a
        args.append(nc.dram_tensor(f"in_{name}_dram", a.shape, _mybir.dt.from_np(a.dtype), kind="ExternalInput").ap())
    shape = tuple(inputs["x"].shape)
    out = nc.dram_tensor("out_0_dram", shape, _mybir.dt.float32, kind="ExternalOutput").ap()
    graph_kernel(nc, *args, out)
    r = _run(nc, [arrays], core_ids=[0])
    return r.results[0]["out_0_dram"]
```
